# Optimizing a Trainium2 kernel written in Bass

```python
import numpy as np
import jax
import jax.numpy as jnp

def _softmax(x, axis=-1):
    return jax.nn.softmax(x, axis=axis)

def _gelu(x):
    return jax.nn.gelu(x, approximate=True)

def _silu(x):
    return jax.nn.silu(x)

def _sigmoid(x):
    return jax.nn.sigmoid(x)

def _layernorm(x, axis=-1, eps=1e-05):
    m = jnp.mean(x, axis=axis, keepdims=True)
    v = jnp.var(x, axis=axis, keepdims=True)
    return (x - m) / jnp.sqrt(v + eps)

def _scatter_add(tgt, idx, src, axis=0):
    return tgt.at[idx].add(src)

def _segment_sum(src, seg, n):
    return jax.ops.segment_sum(src, seg, n)
kernel_name = 'mk_dlrm_tower_d1_rec_r8_0ac960'

def setup_inputs(seed: int=0):
    np.random.seed(seed)
    _w = jnp.asarray

    def _rec_inputs():
        import jax
        import jax.numpy as jnp
        _tk = jax.random.key(seed)
        dense_ctx = jax.random.normal(jax.random.fold_in(_tk, 190), (512, 16), jnp.float32)
        ids = jnp.stack([jax.random.randint(jax.random.fold_in(_tk, 200 + f), (512,), 0, v, jnp.int32) for f, v in enumerate([125000, 1250, 12500, 1000, 1250, 1250, 1000, 1000, 12500, 1000, 12500, 12500, 125000, 12500, 1250, 125000, 12500, 1000, 12500, 125000, 1000, 12500, 12500, 1250, 125000, 12500, 1000, 1000, 12500, 1250, 1250, 125000, 1000, 125000, 12500, 125000, 1250, 1000, 125000])], axis=1)
        tbl_0 = 0.05 * jax.random.normal(jax.random.fold_in(_tk, 500 + 0), (125000, 16), jnp.float32)
        tbl_1 = 0.05 * jax.random.normal(jax.random.fold_in(_tk, 500 + 1), (1250, 16), jnp.float32)
        tbl_2 = 0.05 * jax.random.normal(jax.random.fold_in(_tk, 500 + 2), (12500, 16), jnp.float32)
        tbl_3 = 0.05 * jax.random.normal(jax.random.fold_in(_tk, 500 + 3), (1000, 16), jnp.float32)
        tbl_4 = 0.05 * jax.random.normal(jax.random.fold_in(_tk, 500 + 4), (1250, 16), jnp.float32)
        tbl_5 = 0.05 * jax.random.normal(jax.random.fold_in(_tk, 500 + 5), (1250, 16), jnp.float32)
        tbl_6 = 0.05 * jax.random.normal(jax.random.fold_in(_tk, 500 + 6), (1000, 16), jnp.float32)
        tbl_7 = 0.05 * jax.random.normal(jax.random.fold_in(_tk, 500 + 7), (1000, 16), jnp.float32)
        tbl_8 = 0.05 * jax.random.normal(jax.random.fold_in(_tk, 500 + 8), (12500, 16), jnp.float32)
        tbl_9 = 0.05 * jax.random.normal(jax.random.fold_in(_tk, 500 + 9), (1000, 16), jnp.float32)
        tbl_10 = 0.05 * jax.random.normal(jax.random.fold_in(_tk, 500 + 10), (12500, 16), jnp.float32)
        tbl_11 = 0.05 * jax.random.normal(jax.random.fold_in(_tk, 500 + 11), (12500, 16), jnp.float32)
        tbl_12 = 0.05 * jax.random.normal(jax.random.fold_in(_tk, 500 + 12), (125000, 16), jnp.float32)
        tbl_13 = 0.05 * jax.random.normal(jax.random.fold_in(_tk, 500 + 13), (12500, 16), jnp.float32)
        tbl_14 = 0.05 * jax.random.normal(jax.random.fold_in(_tk, 500 + 14), (1250, 16), jnp.float32)
        tbl_15 = 0.05 * jax.random.normal(jax.random.fold_in(_tk, 500 + 15), (125000, 16), jnp.float32)
        tbl_16 = 0.05 * jax.random.normal(jax.random.fold_in(_tk, 500 + 16), (12500, 16), jnp.float32)
        tbl_17 = 0.05 * jax.random.normal(jax.random.fold_in(_tk, 500 + 17), (1000, 16), jnp.float32)
        tbl_18 = 0.05 * jax.random.normal(jax.random.fold_in(_tk, 500 + 18), (12500, 16), jnp.float32)
        tbl_19 = 0.05 * jax.random.normal(jax.random.fold_in(_tk, 500 + 19), (125000, 16), jnp.float32)
        tbl_20 = 0.05 * jax.random.normal(jax.random.fold_in(_tk, 500 + 20), (1000, 16), jnp.float32)
        tbl_21 = 0.05 * jax.random.normal(jax.random.fold_in(_tk, 500 + 21), (12500, 16), jnp.float32)
        tbl_22 = 0.05 * jax.random.normal(jax.random.fold_in(_tk, 500 + 22), (12500, 16), jnp.float32)
        tbl_23 = 0.05 * jax.random.normal(jax.random.fold_in(_tk, 500 + 23), (1250, 16), jnp.float32)
        tbl_24 = 0.05 * jax.random.normal(jax.random.fold_in(_tk, 500 + 24), (125000, 16), jnp.float32)
        tbl_25 = 0.05 * jax.random.normal(jax.random.fold_in(_tk, 500 + 25), (12500, 16), jnp.float32)
        tbl_26 = 0.05 * jax.random.normal(jax.random.fold_in(_tk, 500 + 26), (1000, 16), jnp.float32)
        tbl_27 = 0.05 * jax.random.normal(jax.random.fold_in(_tk, 500 + 27), (1000, 16), jnp.float32)
        tbl_28 = 0.05 * jax.random.normal(jax.random.fold_in(_tk, 500 + 28), (12500, 16), jnp.float32)
        tbl_29 = 0.05 * jax.random.normal(jax.random.fold_in(_tk, 500 + 29), (1250, 16), jnp.float32)
        tbl_30 = 0.05 * jax.random.normal(jax.random.fold_in(_tk, 500 + 30), (1250, 16), jnp.float32)
        tbl_31 = 0.05 * jax.random.normal(jax.random.fold_in(_tk, 500 + 31), (125000, 16), jnp.float32)
        tbl_32 = 0.05 * jax.random.normal(jax.random.fold_in(_tk, 500 + 32), (1000, 16), jnp.float32)
        tbl_33 = 0.05 * jax.random.normal(jax.random.fold_in(_tk, 500 + 33), (125000, 16), jnp.float32)
        tbl_34 = 0.05 * jax.random.normal(jax.random.fold_in(_tk, 500 + 34), (12500, 16), jnp.float32)
        tbl_35 = 0.05 * jax.random.normal(jax.random.fold_in(_tk, 500 + 35), (125000, 16), jnp.float32)
        tbl_36 = 0.05 * jax.random.normal(jax.random.fold_in(_tk, 500 + 36), (1250, 16), jnp.float32)
        tbl_37 = 0.05 * jax.random.normal(jax.random.fold_in(_tk, 500 + 37), (1000, 16), jnp.float32)
        tbl_38 = 0.05 * jax.random.normal(jax.random.fold_in(_tk, 500 + 38), (125000, 16), jnp.float32)
        _rk = jax.random.fold_in(_tk, 7)
        W_top1 = 0.0606339 * jax.random.normal(jax.random.fold_in(_tk, 801), (272, 512), jnp.float32)
        W_top2 = 0.0441942 * jax.random.normal(jax.random.fold_in(_tk, 802), (512, 256), jnp.float32)
        W_top3 = 0.0625 * jax.random.normal(jax.random.fold_in(_tk, 803), (256, 1), jnp.float32)
        b_top1 = jnp.zeros((512,), jnp.float32)
        b_top2 = jnp.zeros((256,), jnp.float32)
        return (dense_ctx, ids, tbl_0, tbl_1, tbl_2, tbl_3, tbl_4, tbl_5, tbl_6, tbl_7, tbl_8, tbl_9, tbl_10, tbl_11, tbl_12, tbl_13, tbl_14, tbl_15, tbl_16, tbl_17, tbl_18, tbl_19, tbl_20, tbl_21, tbl_22, tbl_23, tbl_24, tbl_25, tbl_26, tbl_27, tbl_28, tbl_29, tbl_30, tbl_31, tbl_32, tbl_33, tbl_34, tbl_35, tbl_36, tbl_37, tbl_38, W_top1, b_top1, W_top2, b_top2, W_top3)
    dense_ctx, ids, tbl_0, tbl_1, tbl_2, tbl_3, tbl_4, tbl_5, tbl_6, tbl_7, tbl_8, tbl_9, tbl_10, tbl_11, tbl_12, tbl_13, tbl_14, tbl_15, tbl_16, tbl_17, tbl_18, tbl_19, tbl_20, tbl_21, tbl_22, tbl_23, tbl_24, tbl_25, tbl_26, tbl_27, tbl_28, tbl_29, tbl_30, tbl_31, tbl_32, tbl_33, tbl_34, tbl_35, tbl_36, tbl_37, tbl_38, W_top1, b_top1, W_top2, b_top2, W_top3 = _rec_inputs()

    def _L0_rec_setup():
        import jax, jax.numpy as jnp
        import numpy as np
        B, F0, D = (256, 39, 16)
        LAYER_SIZES = [128, 128, 128]
        key = jax.random.key(seed)
        ks = jax.random.split(key, 1 + 2 * len(LAYER_SIZES))
        inputs = jax.random.normal(ks[0], (B, F0, D), dtype=jnp.float32)
        out = {'inputs': inputs}
        field_nums = [F0]
        for i, size in enumerate(LAYER_SIZES):
            fk = field_nums[-1]
            fan_in = F0 * fk
            scale = np.sqrt(2.0 / (fan_in + size)).astype(np.float32)
            out[f'w{i}'] = jax.random.normal(ks[1 + 2 * i], (F0, fk, size), dtype=jnp.float32) * scale
            out[f'b{i}'] = jnp.zeros((size,), dtype=jnp.float32)
            field_nums.append(size // 2)
        return out
    _L0_rec_all = _L0_rec_setup()
    _L0_rec_in = {k: v for k, v in _L0_rec_all.items() if k in ('w0', 'w1', 'w2', 'b0', 'b1', 'b2')}
    del _L0_rec_all
    return {'dense_ctx': dense_ctx, 'ids': ids, 'tbl_0': tbl_0, 'tbl_1': tbl_1, 'tbl_2': tbl_2, 'tbl_3': tbl_3, 'tbl_4': tbl_4, 'tbl_5': tbl_5, 'tbl_6': tbl_6, 'tbl_7': tbl_7, 'tbl_8': tbl_8, 'tbl_9': tbl_9, 'tbl_10': tbl_10, 'tbl_11': tbl_11, 'tbl_12': tbl_12, 'tbl_13': tbl_13, 'tbl_14': tbl_14, 'tbl_15': tbl_15, 'tbl_16': tbl_16, 'tbl_17': tbl_17, 'tbl_18': tbl_18, 'tbl_19': tbl_19, 'tbl_20': tbl_20, 'tbl_21': tbl_21, 'tbl_22': tbl_22, 'tbl_23': tbl_23, 'tbl_24': tbl_24, 'tbl_25': tbl_25, 'tbl_26': tbl_26, 'tbl_27': tbl_27, 'tbl_28': tbl_28, 'tbl_29': tbl_29, 'tbl_30': tbl_30, 'tbl_31': tbl_31, 'tbl_32': tbl_32, 'tbl_33': tbl_33, 'tbl_34': tbl_34, 'tbl_35': tbl_35, 'tbl_36': tbl_36, 'tbl_37': tbl_37, 'tbl_38': tbl_38, 'W_top1': W_top1, 'b_top1': b_top1, 'W_top2': W_top2, 'b_top2': b_top2, 'W_top3': W_top3, 'L0_rec_w0': _L0_rec_in['w0'], 'L0_rec_w1': _L0_rec_in['w1'], 'L0_rec_w2': _L0_rec_in['w2'], 'L0_rec_b0': _L0_rec_in['b0'], 'L0_rec_b1': _L0_rec_in['b1'], 'L0_rec_b2': _L0_rec_in['b2']}

def reference(dense_ctx, ids, tbl_0, tbl_1, tbl_2, tbl_3, tbl_4, tbl_5, tbl_6, tbl_7, tbl_8, tbl_9, tbl_10, tbl_11, tbl_12, tbl_13, tbl_14, tbl_15, tbl_16, tbl_17, tbl_18, tbl_19, tbl_20, tbl_21, tbl_22, tbl_23, tbl_24, tbl_25, tbl_26, tbl_27, tbl_28, tbl_29, tbl_30, tbl_31, tbl_32, tbl_33, tbl_34, tbl_35, tbl_36, tbl_37, tbl_38, W_top1, b_top1, W_top2, b_top2, W_top3, L0_rec_w0, L0_rec_w1, L0_rec_w2, L0_rec_b0, L0_rec_b1, L0_rec_b2):
    import jax
    import jax.numpy as jnp

    def _L0_rec_ref(inputs, w0, w1, w2, b0, b1, b2):
        import jax, jax.numpy as jnp
        import numpy as np
        B, F0, D = (256, 39, 16)
        LAYER_SIZES = [128, 128, 128]
        x0 = inputs
        xk = inputs
        params = [(w0, b0), (w1, b1), (w2, b2)]
        n_layers = len(params)
        direct = []
        for idx, (W, b) in enumerate(params):
            z = jnp.einsum('bhd,bkd,hks->bsd', x0, xk, W) + b[None, :, None]
            z = jax.nn.relu(z)
            if idx != n_layers - 1:
                half = z.shape[1] // 2
                xk = z[:, :half, :]
                direct.append(z[:, half:, :])
            else:
                direct.append(z)
        logit = jnp.sum(jnp.concatenate(direct, axis=1), axis=-1)
        return logit
    e = jnp.stack([tbl_0[ids[:, 0]], tbl_1[ids[:, 1]], tbl_2[ids[:, 2]], tbl_3[ids[:, 3]], tbl_4[ids[:, 4]], tbl_5[ids[:, 5]], tbl_6[ids[:, 6]], tbl_7[ids[:, 7]], tbl_8[ids[:, 8]], tbl_9[ids[:, 9]], tbl_10[ids[:, 10]], tbl_11[ids[:, 11]], tbl_12[ids[:, 12]], tbl_13[ids[:, 13]], tbl_14[ids[:, 14]], tbl_15[ids[:, 15]], tbl_16[ids[:, 16]], tbl_17[ids[:, 17]], tbl_18[ids[:, 18]], tbl_19[ids[:, 19]], tbl_20[ids[:, 20]], tbl_21[ids[:, 21]], tbl_22[ids[:, 22]], tbl_23[ids[:, 23]], tbl_24[ids[:, 24]], tbl_25[ids[:, 25]], tbl_26[ids[:, 26]], tbl_27[ids[:, 27]], tbl_28[ids[:, 28]], tbl_29[ids[:, 29]], tbl_30[ids[:, 30]], tbl_31[ids[:, 31]], tbl_32[ids[:, 32]], tbl_33[ids[:, 33]], tbl_34[ids[:, 34]], tbl_35[ids[:, 35]], tbl_36[ids[:, 36]], tbl_37[ids[:, 37]], tbl_38[ids[:, 38]]], axis=1)
    z = _L0_rec_ref(e, L0_rec_w0, L0_rec_w1, L0_rec_w2, L0_rec_b0, L0_rec_b1, L0_rec_b2)
    z = z.reshape(z.shape[0], -1)
    h = jnp.concatenate([z, dense_ctx], axis=1)
    h = jnp.maximum(h @ W_top1 + b_top1, 0.0)
    h = jnp.maximum(h @ W_top2 + b_top2, 0.0)
    y = h @ W_top3
    return y

_drawn_inputs = setup_inputs


def setup_inputs(seed=0):
    import zlib

    import numpy as np

    out = dict(_drawn_inputs(seed))
    spreads = {'b_top1': (0.0, 2.0),
     'b_top2': (0.0, 2.0),
     'L0_rec_b0': (0.0, 0.34),
     'L0_rec_b1': (0.0, 0.545),
     'L0_rec_b2': (0.0, 0.8)}
    factors = {'tbl_0': 8.0,
     'tbl_1': 8.0,
     'tbl_2': 8.0,
     'tbl_3': 8.0,
     'tbl_4': 8.0,
     'tbl_5': 8.0,
     'tbl_6': 8.0,
     'tbl_7': 8.0,
     'tbl_8': 8.0,
     'tbl_9': 8.0,
     'tbl_10': 8.0,
     'tbl_11': 8.0,
     'tbl_12': 8.0,
     'tbl_13': 8.0,
     'tbl_14': 8.0,
     'tbl_15': 8.0,
     'tbl_16': 8.0,
     'tbl_17': 8.0,
     'tbl_18': 8.0,
     'tbl_19': 8.0,
     'tbl_20': 8.0,
     'tbl_21': 8.0,
     'tbl_22': 8.0,
     'tbl_23': 8.0,
     'tbl_24': 8.0,
     'tbl_25': 8.0,
     'tbl_26': 8.0,
     'tbl_27': 8.0,
     'tbl_28': 8.0,
     'tbl_29': 8.0,
     'tbl_30': 8.0,
     'tbl_31': 8.0,
     'tbl_32': 8.0,
     'tbl_33': 8.0,
     'tbl_34': 8.0,
     'tbl_35': 8.0,
     'tbl_36': 8.0,
     'tbl_37': 8.0,
     'tbl_38': 8.0,
     'L0_rec_w0': 8.0,
     'L0_rec_w1': 6.402,
     'L0_rec_w2': 4.94,
     'dense_ctx': 8.0}
    for name, (base, spread) in spreads.items():
        noise = np.random.default_rng([zlib.crc32(name.encode()), seed]).standard_normal(out[name].shape)
        drawn = base * np.exp(spread * noise) if base else spread * noise
        out[name] = jnp.asarray(drawn.astype(out[name].dtype))
    for name, factor in factors.items():
        out[name] = (out[name] * factor).astype(out[name].dtype)
    return out
```

```python
import concourse.bass as bass
from concourse import mybir
from contextlib import ExitStack

BATCH, FIELDS, DIM = 512, 39, 16
PART = 128
OUT = 128
KEEP = OUT // 2
BLOCK = 128
BLOCKS = BATCH // BLOCK
DSTEP = 4
N = DSTEP * BLOCK
CHUNKS = DIM // DSTEP
ROT = FIELDS // 2 + 1
ROT_PER_TILE = PART // FIELDS
T0 = -(-ROT // ROT_PER_TILE)
ROWS0 = ROT_PER_TILE * FIELDS
LAST0 = (ROT - (T0 - 1) * ROT_PER_TILE) * FIELDS
T1 = -(-FIELDS // 2)
WRAP = ROT - 1
GT = 2
G0 = -(-T0 // GT)
G1 = T1 // GT
PER_CHUNK = G0 + 2 * G1
SLOTS = 8
TSLICES = -(-FIELDS * DIM // PART)
XROWS = (FIELDS + WRAP) * DIM
H1, H2, DENSE = 512, 256, 16


def tower(nc, A, fields, out):
    fp32, i32 = mybir.dt.float32, mybir.dt.int32
    ALU, ACT = mybir.AluOpType, mybir.ActivationFunctionType
    RELU = ACT.Relu

    with ExitStack() as ctx:
        def sb(name, shape, dt=fp32):
            return ctx.enter_context(nc.sbuf_tensor(name, shape, dt))

        def bank(name):
            return ctx.enter_context(nc.psum_tensor(name, [PART, N], fp32))

        def sem(name):
            return ctx.enter_context(nc.semaphore(name))

        w0 = sb("w0", [PART, T0, OUT])
        w0_rev = sb("w0_rev", [PART, T0, OUT])
        w1 = sb("w1", [PART, T1, OUT])
        w2 = sb("w2", [PART, T1, OUT])
        wt1 = sb("wt1", [PART, 2, H1])
        wt1_dense = sb("wt1_dense", [DENSE, H1])
        wt2 = sb("wt2", [PART, H1 // PART, H2])
        wt3 = sb("wt3", [PART, H2 // PART])
        bias = sb("bias", [PART, 3])
        bt1 = sb("bt1", [PART, H1 // PART])
        bt2 = sb("bt2", [PART, H2 // PART])
        ident = sb("ident", [PART, PART])
        ids_all = sb("ids_all", [PART, BLOCKS, FIELDS], i32)
        idx = sb("idx", [PART, FIELDS], i32)
        rows = sb("rows", [PART, FIELDS * DIM])
        xt = sb("xt", [PART, TSLICES, BLOCK])
        rot = [sb(f"rot{n}", [ROWS0, T0, N]) for n in range(2)]
        rep = [sb(f"rep{n}", [ROWS0, N]) for n in range(2)]
        bc = [sb(f"bc{n}", [PART, T1, N]) for n in range(2)]
        prod = sb("prod", [PART, SLOTS, GT, N])
        direct = [sb(f"direct{n}", [PART, 2, N]) for n in range(2)]
        total = sb("total", [PART, 2, N])
        half = sb("half", [PART, 2, N // 2])
        logits = sb("logits", [PART, 2, BATCH])
        dense = sb("dense", [PART, BLOCKS, DENSE])
        denseT = sb("denseT", [DENSE, BATCH])
        h1 = prod[:, 0:2].rearrange("p a b n -> p (a b) n")
        h2 = prod[:, 2]
        y = prod[0:1, 3, 0]

        z = [bank(f"z{n}") for n in range(3)]
        xk = [bank(f"xk{n}") for n in range(2)]
        tp = [bank(f"tp{n}") for n in range(2)]
        top = bank("top")

        ids_in = sem("ids_in")
        w0_in = sem("w0_in")
        w12_in = sem("w12_in")
        small_in = sem("small_in")
        top_in = sem("top_in")
        ident_zero = sem("ident_zero")
        ident_ready = sem("ident_ready")
        w0_ready = sem("w0_ready")
        idx_ready = sem("idx_ready")
        gathered = sem("gathered")
        transposed = sem("transposed")
        xt_ready = sem("xt_ready")
        stored = sem("stored")
        rot_free = sem("rot_free")
        bc_free = sem("bc_free")
        rot_in = [sem(f"rot_in{n}") for n in range(2)]
        bc_first = [sem(f"bc_first{n}") for n in range(2)]
        bc_second = [sem(f"bc_second{n}") for n in range(2)]
        slot_free = sem("slot_free")
        prod_ready = sem("prod_ready")
        z_done = [sem(f"z_done{n}") for n in range(3)]
        z_read = [sem(f"z_read{n}") for n in range(3)]
        x_ready = [sem(f"x_ready{n}") for n in range(2)]
        x_read = [sem(f"x_read{n}") for n in range(2)]
        direct_free = sem("direct_free")
        summed = sem("summed")
        half_ready = sem("half_ready")
        logits_ready = sem("logits_ready")
        dense_t = sem("dense_t")
        dense_ready = sem("dense_ready")
        h1_done = sem("h1_done")
        h1_ready = sem("h1_ready")
        h2_done = sem("h2_done")
        h2_ready = sem("h2_ready")
        y_done = sem("y_done")
        y_ready = sem("y_ready")
        written = sem("written")
        pool_step = sem("pool_step")

        block = ctx.enter_context(nc.Block())

        ROW = DIM * BLOCK
        FBLOCK = XROWS * BLOCK
        HALF_T = T1 // 2

        @block.sync
        def _(sp):
            sp.dma_start(ids_all[:, :, :], A["ids"].rearrange("(j p) f -> p j f", p=BLOCK)).then_inc(ids_in, 16)
            full = (T0 - 1) * ROWS0
            for src, dst in ((A["w0_fwd"], w0), (A["w0_rev"], w0_rev)):
                sp.dma_start(dst[0:ROWS0, 0:T0 - 1, :], src[0:full, :].rearrange("(t p) s -> p t s", p=ROWS0)).then_inc(w0_in, 16)
                sp.dma_start(dst[0:LAST0, T0 - 1, :], src[full:full + LAST0, :]).then_inc(w0_in, 16)
            for name, dst in (("L0_rec_w1", w1), ("L0_rec_w2", w2)):
                flat = A[name].rearrange("h k s -> (h k) s")
                body = (T1 - 1) * PART
                sp.dma_start(dst[:, 0:T1 - 1, :], flat[0:body, :].rearrange("(t p) s -> p t s", p=PART)).then_inc(w12_in, 16)
                sp.dma_start(dst[0:KEEP, T1 - 1, :], flat[body:body + KEEP, :]).then_inc(w12_in, 16)

            with sp.Fori(0, BLOCKS) as i:
                sp.wait_ge(stored, (i + 1) * 64)
                for q in range(CHUNKS):
                    b = q % 2
                    at = i * FBLOCK + q * N
                    sp.wait_ge(rot_free, i * CHUNKS + (q + 1))
                    for r in range(ROT_PER_TILE):
                        tiles = len(range(r, ROT, ROT_PER_TILE))
                        src = bass.AP(fields.tensor, at + r * ROW, [[ROW, FIELDS], [ROT_PER_TILE * ROW, tiles], [1, N]])
                        sp.dma_start(rot[b][r * FIELDS:(r + 1) * FIELDS, 0:tiles, :], src).then_inc(rot_in[b], 16)
                        src = bass.AP(fields.tensor, at, [[ROW, FIELDS], [1, N]])
                        sp.dma_start(rep[b][r * FIELDS:(r + 1) * FIELDS, :], src).then_inc(rot_in[b], 16)
                    sp.wait_ge(bc_free, i * CHUNKS + (q + 1))
                    for first, arrived in ((0, bc_first[b]), (HALF_T, bc_second[b])):
                        for parity in range(2):
                            tiles = len(range(2 * first + parity, min(FIELDS, 2 * (first + HALF_T)), 2))
                            src = bass.AP(fields.tensor, at + (2 * first + parity) * ROW, [[0, KEEP], [2 * ROW, tiles], [1, N]])
                            sp.dma_start(bc[b][parity * KEEP:(parity + 1) * KEEP, first:first + tiles, :], src).then_inc(arrived, 16)
            sp.wait_ge(y_ready, 1)
            sp.dma_start(out.rearrange("(a b) c -> a (b c)", a=1), y).then_inc(written, 16)
            sp.wait_ge(written, 16)

        @block.gpsimd
        def _(pool):
            pool.memset(ident[:, :], 0.0).then_inc(ident_zero, 1)
            pool.wait_ge(ident_zero, 1)
            pool.affine_select(out=ident[:, :], in_=ident[:, :], compare_op=ALU.not_equal, fill=1.0,
                               base=0, pattern=[[-1, PART]], channel_multiplier=1).then_inc(ident_ready, 1)
            pool.wait_ge(ids_in, 16)

            def gather(first, last):
                for f in range(first, last):
                    pool.indirect_dma_start(rows[:, f * DIM:(f + 1) * DIM], None, A[f"tbl_{f}"],
                                            bass.IndirectOffsetOnAxis(idx[:, f:f + 1], 0)).then_inc(gathered, 16)

            pool.tensor_copy(idx[:, :], ids_all[:, 0, :]).then_inc(idx_ready, 1)
            pool.wait_ge(idx_ready, 1)
            gather(0, FIELDS)

            def body(i, last):
                if not last:
                    pool.wait_ge(gathered, (i + 1) * (16 * FIELDS))
                    pool.sem_inc(pool_step, 1)
                    pool.tensor_copy(idx[:, :], ids_all[:, i + 1, :]).then_inc(idx_ready, 1)
                    pool.wait_ge(idx_ready, i + 2)
                    pool.wait_ge(transposed, i + 1)
                    pool.sem_inc(pool_step, 1)
                    gather(0, FIELDS // 2)
                for q in range(CHUNKS):
                    for layer in range(3):
                        pool.wait_ge(z_read[layer], i * CHUNKS + (q + 2))
                    pool.wait_ge(summed, i * (CHUNKS + 2) + (q + 2))
                    pool.sem_inc(pool_step, 1)
                    if q == 0:
                        ins = pool.tensor_copy(total[:, :, :], direct[q % 2][:, :, :])
                    else:
                        ins = pool.tensor_tensor(total[:, :, :], total[:, :, :], direct[q % 2][:, :, :], ALU.add)
                    ins.then_inc(summed, 1)
                    pool.wait_ge(summed, i * (CHUNKS + 2) + (q + 3))
                    pool.sem_inc(direct_free, 1)
                    if q == 0 and not last:
                        gather(FIELDS // 2, FIELDS)
                pool.tensor_tensor(half[:, :, :], total[:, :, 0:N // 2], total[:, :, N // 2:N], ALU.add).then_inc(summed, 1)
                pool.wait_ge(summed, i * (CHUNKS + 2) + (CHUNKS + 3))
                pool.tensor_tensor(logits[:, :, bass.ds(i * BLOCK, BLOCK)], half[:, :, 0:BLOCK], half[:, :, BLOCK:2 * BLOCK], ALU.add).then_inc(summed, 1)

            pool.sem_inc(summed, 2)
            with pool.Fori(0, BLOCKS - 1) as i:
                body(i, False)
            body(BLOCKS - 1, True)
            pool.wait_ge(summed, BLOCKS * (CHUNKS + 2) + 2)
            pool.sem_inc(logits_ready, 1)

        @block.scalar
        def _(act):
            for layer in range(3):
                act.dma_start(bias[:, layer:layer + 1], A[f"L0_rec_b{layer}"].rearrange("(s a) -> s a", a=1)).then_inc(small_in, 16)
            act.dma_start(dense[:, :, :], A["dense_ctx"].rearrange("(j p) c -> p j c", p=BLOCK)).then_inc(small_in, 16)
            act.dma_start(wt1[:, :, :], A["W_top1"][0:2 * OUT, :].rearrange("(t p) n -> p t n", p=PART)).then_inc(top_in, 16)
            act.dma_start(wt1_dense[:, :], A["W_top1"][2 * OUT:2 * OUT + DENSE, :]).then_inc(top_in, 16)
            act.dma_start(wt2[:, :, :], A["W_top2"].rearrange("(t p) n -> p t n", p=PART)).then_inc(top_in, 16)
            with nc.allow_non_contiguous_dma(reason="small columns"):
                act.dma_start(wt3[:, :], A["W_top3"].rearrange("(t p) n -> p (t n)", p=PART)).then_inc(top_in, 16)
                act.dma_start(bt1[:, :], A["b_top1"].rearrange("(t p) -> p t", p=PART)).then_inc(top_in, 16)
                act.dma_start(bt2[:, :], A["b_top2"].rearrange("(t p) -> p t", p=PART)).then_inc(top_in, 16)

            def store_block(i):
                act.wait_ge(transposed, i + 1)
                act.activation(xt[:, 0:4, :].rearrange("p t n -> p (t n)"), tp[0][:, :], ACT.Copy).then_inc(xt_ready, 1)
                act.activation(xt[0:FIELDS * DIM - 4 * PART, 4, :], tp[1][0:FIELDS * DIM - 4 * PART, 0:BLOCK], ACT.Copy).then_inc(xt_ready, 1)
                act.wait_ge(xt_ready, i * 2 + 2)
                at = i * FBLOCK
                tail = FIELDS * DIM - 4 * PART
                act.dma_start(bass.AP(fields.tensor, at, [[BLOCK, PART], [PART * BLOCK, 4], [1, BLOCK]]), xt[:, 0:4, :]).then_inc(stored, 16)
                act.dma_start(bass.AP(fields.tensor, at + 4 * PART * BLOCK, [[BLOCK, tail], [1, BLOCK]]), xt[0:tail, 4, :]).then_inc(stored, 16)
                wrap = at + FIELDS * DIM * BLOCK
                left = WRAP * DIM - 2 * PART
                act.dma_start(bass.AP(fields.tensor, wrap, [[BLOCK, PART], [PART * BLOCK, 2], [1, BLOCK]]), xt[:, 0:2, :]).then_inc(stored, 16)
                act.dma_start(bass.AP(fields.tensor, wrap + 2 * PART * BLOCK, [[BLOCK, left], [1, BLOCK]]), xt[0:left, 2, :]).then_inc(stored, 16)

            def kept(layer, c):
                act.wait_ge(z_done[layer], c + 1)
                act.wait_ge(x_read[layer], c + 1)
                act.activation(xk[layer][0:KEEP, :], z[layer][0:KEEP, :], RELU, bias=bias[0:KEEP, layer:layer + 1]).then_inc(x_ready[layer], 1)
                act.activation(xk[layer][KEEP:OUT, :], z[layer][0:KEEP, :], RELU, bias=bias[0:KEEP, layer:layer + 1]).then_inc(x_ready[layer], 1)

            def layer0_out(c, b):
                kept(0, c)
                act.wait_ge(direct_free, c + 1)
                act.activation(direct[b][0:KEEP, 0, :], z[0][KEEP:OUT, :], RELU, bias=bias[KEEP:OUT, 0:1]).then_inc(z_read[0], 1)

            def layer1_out(c, b):
                kept(1, c)
                act.activation(direct[b][KEEP:OUT, 0, :], z[1][KEEP:OUT, :], RELU, bias=bias[KEEP:OUT, 1:2]).then_inc(z_read[1], 1)

            def layer2_out(c, b):
                act.wait_ge(z_done[2], c + 1)
                act.activation(direct[b][:, 1, :], z[2][:, :], RELU, bias=bias[:, 2:3]).then_inc(z_read[2], 1)

            def body(i, last):
                for q in range(CHUNKS):
                    c = i * CHUNKS + q
                    if q == 2 and not last:
                        store_block(i + 1)
                    layer1_out(c, q % 2)
                    if not (last and q == CHUNKS - 1):
                        layer0_out(c + 1, (q + 1) % 2)
                    layer2_out(c, q % 2)

            act.wait_ge(small_in, 64)
            store_block(0)
            act.wait_ge(dense_t, 1)
            act.activation(denseT[:, :], top[0:DENSE, :], ACT.Copy).then_inc(dense_ready, 1)
            layer0_out(0, 0)
            with act.Fori(0, BLOCKS - 1) as i:
                body(i, False)
            body(BLOCKS - 1, True)

            act.wait_ge(top_in, 16 * 6)
            for m in range(H1 // PART):
                act.wait_ge(h1_done, m + 1)
                act.activation(h1[:, m, :], (top, tp[0], tp[1], z[0])[m][:, :], RELU, bias=bt1[:, m:m + 1]).then_inc(h1_ready, 1)
            for m in range(H2 // PART):
                act.wait_ge(h2_done, m + 1)
                act.activation(h2[:, m, :], (z[1], z[2])[m][:, :], RELU, bias=bt2[:, m:m + 1]).then_inc(h2_ready, 1)
            act.wait_ge(y_done, 1)
            act.activation(y, xk[0][0:1, :], ACT.Copy).then_inc(y_ready, 1)

        @block.vector
        def _(dve):
            dve.wait_ge(w0_in, 64)
            nc.vector.tensor_tensor(w0[0:ROWS0, 0:T0 - 1, :], w0[0:ROWS0, 0:T0 - 1, :], w0_rev[0:ROWS0, 0:T0 - 1, :], ALU.add).then_inc(w0_ready, 1)
            nc.vector.tensor_tensor(w0[0:LAST0, T0 - 1, :], w0[0:LAST0, T0 - 1, :], w0_rev[0:LAST0, T0 - 1, :], ALU.add).then_inc(w0_ready, 1)
            dve.sem_inc(slot_free, SLOTS)
            dve.sem_inc(rot_free, 2)
            dve.sem_inc(bc_free, 2)
            dve.sem_inc(direct_free, 2)
            dve.sem_inc(x_read[0], 1)
            dve.sem_inc(x_read[1], 1)

            def layer0_products(g0, c, b, fills):
                dve.wait_ge(rot_in[b], fills * 96)
                for g in range(G0):
                    slot = (g0[1] + g) % SLOTS
                    dve.wait_ge(slot_free, g0[0] + (g + 1))
                    if g < G0 - 1:
                        ins = nc.vector.tensor_tensor(prod[0:ROWS0, slot], rot[b][:, GT * g:GT * g + GT, :],
                                                      rep[b][:, None, :].to_broadcast([ROWS0, GT, N]), ALU.mult)
                    else:
                        ins = nc.vector.tensor_tensor(prod[0:LAST0, slot, 0], rot[b][0:LAST0, T0 - 1, :], rep[b][0:LAST0, :], ALU.mult)
                    ins.then_inc(prod_ready, 1)
                dve.wait_ge(prod_ready, g0[0] + G0)
                dve.sem_inc(rot_free, 1)

            def field_products(g0, c, b, layer, fills):
                dve.wait_ge(x_ready[layer - 1], c * 2 + 2)
                for g in range(G1):
                    slot = (g0[1] + g) % SLOTS
                    if layer == 1 and g == 0:
                        dve.wait_ge(bc_first[b], fills * 32)
                    if layer == 1 and g == G1 // 2:
                        dve.wait_ge(bc_second[b], fills * 32)
                    dve.wait_ge(slot_free, g0[0] + (g + 1))
                    if g < G1 - 1:
                        ins = nc.vector.tensor_tensor(prod[:, slot], bc[b][:, GT * g:GT * g + GT, :],
                                                      xk[layer - 1][:, None, :].to_broadcast([PART, GT, N]), ALU.mult)
                    else:
                        nc.vector.tensor_tensor(prod[:, slot, 0], bc[b][:, T1 - 2, :], xk[layer - 1][:, :], ALU.mult)
                        ins = nc.vector.tensor_tensor(prod[0:KEEP, slot, 1], bc[b][0:KEEP, T1 - 1, :], xk[layer - 1][0:KEEP, :], ALU.mult)
                    ins.then_inc(prod_ready, 1)
                dve.wait_ge(prod_ready, g0[0] + G1)
                dve.sem_inc(x_read[layer - 1], 1)
                if layer == 2:
                    dve.sem_inc(bc_free, 1)

            def body(i, last):
                for q in range(CHUNKS):
                    c = i * CHUNKS + q
                    st = G0 + q * PER_CHUNK
                    first = (i * (CHUNKS * PER_CHUNK) + st)
                    field_products((first, st), c, q % 2, 1, i * 2 + (q // 2 + 1))
                    if not (last and q == CHUNKS - 1):
                        n = q + 1
                        layer0_products((first + G1, st + G1), c + 1, n % 2, i * 2 + (n // 2 + 1))
                    skip = 0 if (last and q == CHUNKS - 1) else G0
                    field_products((first + (G1 + skip), st + G1 + skip), c, q % 2, 2, 0)

            layer0_products((0, 0), 0, 0, 1)
            with dve.Fori(0, BLOCKS - 1) as i:
                body(i, False)
            body(BLOCKS - 1, True)

        @block.tensor
        def _(pe):
            def transposes(i, first=False):
                pe.wait_ge(gathered, (i + 1) * (16 * FIELDS))
                if not first:
                    pe.wait_ge(xt_ready, i * 2)
                for t in range(TSLICES):
                    m = min(PART, FIELDS * DIM - t * PART)
                    dst = tp[0][0:m, t * BLOCK:(t + 1) * BLOCK] if t < 4 else tp[1][0:m, 0:BLOCK]
                    ins = nc.tensor.transpose(dst, rows[:, t * PART:t * PART + m], ident[:, :])
                ins.then_inc(transposed, 1)

            def layer0(g0, c):
                pe.wait_ge(z_read[0], c + 1)
                for g in range(G0):
                    slot = (g0[1] + g) % SLOTS
                    pe.wait_ge(prod_ready, g0[0] + (g + 1))
                    for t in range(GT * g, min(T0, GT * g + GT)):
                        k = ROWS0 if t < T0 - 1 else LAST0
                        ins = nc.tensor.matmul(z[0][:, :], w0[0:k, t, :], prod[0:k, slot, t - GT * g], start=(t == 0), stop=(t == T0 - 1))
                    ins.then_inc(slot_free, 1)
                pe.wait_ge(slot_free, g0[0] + (G0 + SLOTS))
                pe.sem_inc(z_done[0], 1)

            def fields_layer(g0, c, layer, w):
                pe.wait_ge(z_read[layer], c + 1)
                for g in range(G1):
                    slot = (g0[1] + g) % SLOTS
                    pe.wait_ge(prod_ready, g0[0] + (g + 1))
                    for t in range(GT * g, GT * g + GT):
                        k = PART if t < T1 - 1 else KEEP
                        ins = nc.tensor.matmul(z[layer][:, :], w[0:k, t, :], prod[0:k, slot, t - GT * g], start=(t == 0), stop=(t == T1 - 1))
                    ins.then_inc(slot_free, 1)
                pe.wait_ge(slot_free, g0[0] + (G1 + SLOTS))
                pe.sem_inc(z_done[layer], 1)

            def body(i, last):
                for q in range(CHUNKS):
                    c = i * CHUNKS + q
                    st = G0 + q * PER_CHUNK
                    first = i * (CHUNKS * PER_CHUNK) + st
                    if q == 2 and not last:
                        transposes(i + 1)
                    fields_layer((first, st), c, 1, w1)
                    if not (last and q == CHUNKS - 1):
                        layer0((first + G1, st + G1), c + 1)
                    skip = 0 if (last and q == CHUNKS - 1) else G0
                    fields_layer((first + (G1 + skip), st + G1 + skip), c, 2, w2)

            for layer in range(3):
                pe.sem_inc(z_read[layer], 1)
            pe.wait_ge(ident_ready, 1)
            pe.wait_ge(small_in, 64)
            for j in range(BLOCKS):
                ins = nc.tensor.transpose(top[0:DENSE, j * BLOCK:(j + 1) * BLOCK], dense[:, j, :], ident[:, :])
            ins.then_inc(dense_t, 1)
            transposes(0, first=True)
            pe.wait_ge(w0_ready, 2)
            layer0((0, 0), 0)
            pe.wait_ge(w12_in, 64)
            with pe.Fori(0, BLOCKS - 1) as i:
                body(i, False)
            body(BLOCKS - 1, True)

            pe.wait_ge(top_in, 16 * 6)
            pe.wait_ge(dense_ready, 1)
            pe.wait_ge(logits_ready, 1)
            pe.wait_ge(xt_ready, 2 * BLOCKS)
            pe.wait_ge(z_read[0], BLOCKS * CHUNKS + 1)
            for m in range(H1 // PART):
                dst = (top, tp[0], tp[1], z[0])[m]
                for t in range(2):
                    nc.tensor.matmul(dst[:, :], wt1[:, t, m * PART:(m + 1) * PART], logits[:, t, :], start=(t == 0), stop=False)
                nc.tensor.matmul(dst[:, :], wt1_dense[:, m * PART:(m + 1) * PART], denseT[:, :], start=False, stop=True).then_inc(h1_done, 1)
            pe.wait_ge(h1_ready, H1 // PART)
            for layer in (1, 2):
                pe.wait_ge(z_read[layer], BLOCKS * CHUNKS + 1)
            for m in range(H2 // PART):
                for t in range(H1 // PART):
                    ins = nc.tensor.matmul((z[1], z[2])[m][:, :], wt2[:, t, m * PART:(m + 1) * PART], h1[:, t, :], start=(t == 0), stop=(t == H1 // PART - 1))
                ins.then_inc(h2_done, 1)
            pe.wait_ge(h2_ready, H2 // PART)
            pe.wait_ge(x_read[0], BLOCKS * CHUNKS + 1)
            for t in range(H2 // PART):
                ins = nc.tensor.matmul(xk[0][0:1, :], wt3[:, t:t + 1], h2[:, t, :], start=(t == 0), stop=(t == H2 // PART - 1))
            ins.then_inc(y_done, 1)


def kernel(**inputs):
    import numpy as _np
    import concourse.bacc as _bacc
    from concourse import mybir as _mybir
    from concourse.bass_utils import run_bass_kernel_spmd as _run

    nc = _bacc.Bacc("TRN2", target_bir_lowering=False, num_devices=1)
    given = {k: _np.ascontiguousarray(v) for k, v in inputs.items() if k != "L0_rec_w0"}
    w0 = _np.asarray(inputs["L0_rec_w0"])
    r, i = _np.arange(ROT)[:, None], _np.arange(FIELDS)[None, :]
    j = (i + r) % FIELDS
    given["w0_fwd"] = _np.ascontiguousarray(w0[i + 0 * r, j].reshape(ROT * FIELDS, OUT))
    rev = w0[j, i + 0 * r].reshape(ROT * FIELDS, OUT).copy()
    rev[0:FIELDS] = 0
    given["w0_rev"] = rev
    arrays, aps = {}, {}
    for name, a in given.items():
        arrays["in_" + name] = a
        aps[name] = nc.dram_tensor("in_" + name, a.shape, _mybir.dt.from_np(a.dtype), kind="ExternalInput").ap()
    fields = nc.dram_tensor("fields", (BLOCKS * XROWS * BLOCK,), _mybir.dt.float32).ap()
    out = nc.dram_tensor("out_y", (BATCH, 1), _mybir.dt.float32, kind="ExternalOutput").ap()
    tower(nc, aps, fields, out)
    result = _run(nc, [arrays], core_ids=[0])
    return result.results[0]["out_y"]
```

```python
import concourse.bass as bass
from concourse import mybir
from contextlib import ExitStack

BATCH, FIELDS, DIM = 512, 39, 16
PART = 128
OUT = 128
KEEP = OUT // 2
BLOCK = 128
BLOCKS = BATCH // BLOCK
DSTEP = 4
N = DSTEP * BLOCK
CHUNKS = DIM // DSTEP
ROT = FIELDS // 2 + 1
ROT_PER_TILE = PART // FIELDS
T0 = -(-ROT // ROT_PER_TILE)
ROWS0 = ROT_PER_TILE * FIELDS
LAST0 = (ROT - (T0 - 1) * ROT_PER_TILE) * FIELDS
T1 = -(-FIELDS // 2)
WRAP = ROT - 1
GT = 2
G0 = -(-T0 // GT)
G1 = T1 // GT
SPLIT = {0: (), 1: (1, 3, 5, 7), 2: (1, 4, 7)}
WHOLE_CHUNK = G0 + 2 * G1 - sum(map(len, SPLIT.values()))
SPLIT_CHUNK = sum(map(len, SPLIT.values()))
WHOLE_SLOTS = 4
RAW_SLOTS = 2
PART_SLOTS = 4
LAG = 2
SECTION = 4
SECTIONS = T1 // SECTION
TSLICES = -(-FIELDS * DIM // PART)
XROWS = (FIELDS + WRAP) * DIM
H1, H2, DENSE = 512, 256, 16


def tower(nc, A, fields, out):
    fp32, fp32r, i32 = mybir.dt.float32, mybir.dt.float32r, mybir.dt.int32
    ALU, ACT = mybir.AluOpType, mybir.ActivationFunctionType
    RELU = ACT.Relu

    with ExitStack() as ctx:
        def sb(name, shape, dt=fp32):
            return ctx.enter_context(nc.sbuf_tensor(name, shape, dt))

        def bank(name):
            return ctx.enter_context(nc.psum_tensor(name, [PART, N], fp32))

        def sem(name):
            return ctx.enter_context(nc.semaphore(name))

        w0 = sb("w0", [PART, T0, OUT])
        w1 = sb("w1", [PART, T1, OUT])
        w2 = sb("w2", [PART, T1, OUT])
        w_high = sb("w_high", [PART, GT * SPLIT_CHUNK + 2, OUT], fp32r)
        w_low = sb("w_low", [PART, GT * SPLIT_CHUNK + 2, OUT], fp32r)
        wt3 = sb("wt3", [PART, H2 // PART])
        bias = sb("bias", [PART, 3])
        bt1 = sb("bt1", [PART, H1 // PART])
        bt2 = sb("bt2", [PART, H2 // PART])
        ident = sb("ident", [PART, PART])
        ids_all = sb("ids_all", [PART, BLOCKS, FIELDS], i32)
        idx = sb("idx", [PART, FIELDS], i32)
        rows = sb("rows", [PART, FIELDS * DIM])
        xt = sb("xt", [PART, TSLICES, BLOCK])
        rot = sb("rot", [ROWS0, T0, N])
        rep = sb("rep", [ROWS0, N])
        bc = sb("bc", [PART, T1, N])
        whole = sb("whole", [PART, WHOLE_SLOTS, GT, N])
        raw = sb("raw", [PART, RAW_SLOTS, GT, N])
        high = sb("high", [PART, PART_SLOTS, GT, N], fp32r)
        low = sb("low", [PART, PART_SLOTS, GT, N], fp32r)
        stack_raw = sb("stack_raw", [PART, N])
        stack = sb("stack", [PART, N], fp32r)
        direct = [sb(f"direct{n}", [PART, 2, N]) for n in range(2)]
        total = sb("total", [PART, 2, N])
        half = sb("half", [PART, 2, N // 2])
        logits = sb("logits", [PART, 2, BATCH])
        dense = sb("dense", [PART, BLOCKS, DENSE])
        denseT = sb("denseT", [DENSE, BATCH])
        w0_rev = whole[:, 0:2].rearrange("p a b n -> p (a b n)")[:, 0:T0 * OUT].rearrange("p (t s) -> p t s", s=OUT)
        wt1 = bc[:, 0:2, :]
        wt1_dense = bc[0:DENSE, 2, :]
        wt2 = bc[:, 3:5, :].rearrange("p a (b n) -> p (a b) n", n=H2)
        h1 = whole[:, 0:2].rearrange("p a b n -> p (a b) n")
        h2 = whole[:, 2]
        y = whole[0:1, 3, 0]

        z = [bank(f"z{n}") for n in range(3)]
        xk = [bank(f"xk{n}") for n in range(2)]
        tp = [bank(f"tp{n}") for n in range(2)]
        top = bank("top")

        ids_in = sem("ids_in")
        w0_in = sem("w0_in")
        w12_in = sem("w12_in")
        small_in = sem("small_in")
        top_in = sem("top_in")
        ident_zero = sem("ident_zero")
        ident_ready = sem("ident_ready")
        w0_ready = sem("w0_ready")
        idx_ready = sem("idx_ready")
        gathered = sem("gathered")
        transposed = sem("transposed")
        xt_ready = sem("xt_ready")
        stored = sem("stored")
        rot_free = sem("rot_free")
        bc_free = sem("bc_free")
        rot_in = sem("rot_in")
        bc_in = [sem(f"bc_in{n}") for n in range(SECTIONS)]
        whole_ready = sem("whole_ready")
        whole_free = sem("whole_free")
        raw_ready = sem("raw_ready")
        high_ready = sem("high_ready")
        low_ready = sem("low_ready")
        parts_free = sem("parts_free")
        stack_ready = sem("stack_ready")
        stack_high = sem("stack_high")
        stack_low = sem("stack_low")
        stack_free = sem("stack_free")
        w_split = sem("w_split")
        sp_step = sem("sp_step")
        z_read = [sem(f"z_read{n}") for n in range(3)]
        x_ready = [sem(f"x_ready{n}") for n in range(2)]
        direct_free = sem("direct_free")
        summed = sem("summed")
        half_ready = sem("half_ready")
        logits_ready = sem("logits_ready")
        dense_t = sem("dense_t")
        dense_ready = sem("dense_ready")
        h1_done = sem("h1_done")
        h1_ready = sem("h1_ready")
        h2_done = sem("h2_done")
        h2_ready = sem("h2_ready")
        y_done = sem("y_done")
        y_ready = sem("y_ready")
        written = sem("written")
        pool_step = sem("pool_step")

        block = ctx.enter_context(nc.Block())

        ROW = DIM * BLOCK
        FBLOCK = XROWS * BLOCK

        STEP = [(1, g) for g in range(G1)] + [(0, g) for g in range(G0)] + [(2, g) for g in range(G1)]

        def is_split(layer, g):
            return g in SPLIT[layer]

        def number(layer, g, final):
            kind = is_split(layer, g)
            before = STEP[:STEP.index((layer, g))]
            n = sum(is_split(*x) == kind for x in before)
            return n - (G0 if final and layer == 2 and not kind else 0)

        def whole_at(c, layer, g, final=False):
            return c * WHOLE_CHUNK + (G0 + number(layer, g, final))

        def split_at(c, layer, g):
            return c * SPLIT_CHUNK + number(layer, g, False)

        SPLIT_GROUPS = [x for x in STEP if is_split(*x)]
        HEAD = 1
        HEAD2 = 1
        split_weights = [(GT * n + u, (w1, w2)[layer - 1], GT * g + u)
                         for n, (layer, g) in enumerate(SPLIT_GROUPS) for u in range(GT)]
        split_weights += [(GT * SPLIT_CHUNK + n, w, T1 - 1) for n, w in enumerate((w1, w2))]

        @block.sync
        def _(sp):
            sp.dma_start(ids_all[:, :, :], A["ids"].rearrange("(j p) f -> p j f", p=BLOCK)).then_inc(ids_in, 16)
            full = (T0 - 1) * ROWS0
            for src, dst in ((A["w0_fwd"], w0), (A["w0_rev"], w0_rev)):
                sp.dma_start(dst[0:ROWS0, 0:T0 - 1, :], src[0:full, :].rearrange("(t p) s -> p t s", p=ROWS0)).then_inc(w0_in, 16)
                sp.dma_start(dst[0:LAST0, T0 - 1, :], src[full:full + LAST0, :]).then_inc(w0_in, 16)
            for name, dst in (("L0_rec_w1", w1), ("L0_rec_w2", w2)):
                flat = A[name].rearrange("h k s -> (h k) s")
                body = (T1 - 1) * PART
                sp.dma_start(dst[:, 0:T1 - 1, :], flat[0:body, :].rearrange("(t p) s -> p t s", p=PART)).then_inc(w12_in, 16)
                for part in range(2):
                    sp.dma_start(dst[part * KEEP:(part + 1) * KEEP, T1 - 1, :], flat[body:body + KEEP, :]).then_inc(w12_in, 16)

            def load_rotations(at):
                for r in range(ROT_PER_TILE):
                    tiles = len(range(r, ROT, ROT_PER_TILE))
                    src = bass.AP(fields.tensor, at + r * ROW, [[ROW, FIELDS], [ROT_PER_TILE * ROW, tiles], [1, N]])
                    sp.dma_start(rot[r * FIELDS:(r + 1) * FIELDS, 0:tiles, :], src).then_inc(rot_in, 16)
                    src = bass.AP(fields.tensor, at, [[ROW, FIELDS], [1, N]])
                    sp.dma_start(rep[r * FIELDS:(r + 1) * FIELDS, :], src).then_inc(rot_in, 16)

            def load_broadcasts(at, c):
                for n in range(SECTIONS):
                    sp.wait_ge(bc_free, c * SECTIONS + (n + 1))
                    for parity in range(2):
                        first = 2 * SECTION * n + parity
                        tiles = len(range(first, min(FIELDS, 2 * SECTION * (n + 1)), 2))
                        src = bass.AP(fields.tensor, at + first * ROW, [[0, KEEP], [2 * ROW, tiles], [1, N]])
                        sp.dma_start(bc[parity * KEEP:(parity + 1) * KEEP, SECTION * n:SECTION * n + tiles, :], src).then_inc(bc_in[n], 16)
                src = bass.AP(fields.tensor, at + (FIELDS - 1) * ROW, [[0, KEEP], [1, N]])
                sp.dma_start(bc[KEEP:PART, T1 - 1, :], src).then_inc(bc_in[SECTIONS - 1], 16)

            def body(i, last):
                for q in range(CHUNKS):
                    c = i * CHUNKS + q
                    load_broadcasts(i * FBLOCK + q * N, c)
                    if q < CHUNKS - 1 or not last:
                        if q == CHUNKS - 1:
                            sp.wait_ge(stored, (i + 2) * 64)
                            sp.sem_inc(sp_step, 1)
                        sp.wait_ge(rot_free, c + 1)
                        sp.sem_inc(sp_step, 1)
                        load_rotations(i * FBLOCK + (q + 1) * N if q < CHUNKS - 1 else (i + 1) * FBLOCK)

            sp.wait_ge(stored, 64)
            load_rotations(0)
            with sp.Fori(0, BLOCKS - 1) as i:
                body(i, False)
            body(BLOCKS - 1, True)
            sp.wait_ge(bc_free, (BLOCKS * CHUNKS + 1) * SECTIONS)
            sp.dma_start(wt1[:, :, :], A["W_top1"][0:2 * OUT, :].rearrange("(t p) n -> p t n", p=PART)).then_inc(top_in, 16)
            sp.dma_start(wt1_dense[:, :], A["W_top1"][2 * OUT:2 * OUT + DENSE, :]).then_inc(top_in, 16)
            sp.dma_start(wt2[:, :, :], A["W_top2"].rearrange("(t p) n -> p t n", p=PART)).then_inc(top_in, 16)
            sp.wait_ge(y_ready, 1)
            sp.dma_start(out.rearrange("(a b) c -> a (b c)", a=1), y).then_inc(written, 16)
            sp.wait_ge(written, 16)

        @block.gpsimd
        def _(pool):
            pool.memset(ident[:, :], 0.0).then_inc(ident_zero, 1)
            pool.wait_ge(ident_zero, 1)
            pool.affine_select(out=ident[:, :], in_=ident[:, :], compare_op=ALU.not_equal, fill=1.0,
                               base=0, pattern=[[-1, PART]], channel_multiplier=1).then_inc(ident_ready, 1)
            pool.wait_ge(ids_in, 16)

            def gather(first, last):
                for f in range(first, last):
                    pool.indirect_dma_start(rows[:, f * DIM:(f + 1) * DIM], None, A[f"tbl_{f}"],
                                            bass.IndirectOffsetOnAxis(idx[:, f:f + 1], 0)).then_inc(gathered, 16)

            pool.tensor_copy(idx[:, :], ids_all[:, 0, :]).then_inc(idx_ready, 1)
            pool.wait_ge(idx_ready, 1)
            gather(0, FIELDS)

            def body(i, last):
                if not last:
                    pool.wait_ge(gathered, (i + 1) * (16 * FIELDS))
                    pool.sem_inc(pool_step, 1)
                    pool.tensor_copy(idx[:, :], ids_all[:, i + 1, :]).then_inc(idx_ready, 1)
                    pool.wait_ge(idx_ready, i + 2)
                    pool.wait_ge(transposed, i + 1)
                    pool.sem_inc(pool_step, 1)
                    gather(0, FIELDS // 2)
                for q in range(CHUNKS):
                    for layer in range(3):
                        pool.wait_ge(z_read[layer], i * CHUNKS + (q + 2))
                    pool.wait_ge(summed, i * (CHUNKS + 2) + (q + 2))
                    pool.sem_inc(pool_step, 1)
                    if q == 0:
                        ins = pool.tensor_copy(total[:, :, :], direct[q % 2][:, :, :])
                    else:
                        ins = pool.tensor_tensor(total[:, :, :], total[:, :, :], direct[q % 2][:, :, :], ALU.add)
                    ins.then_inc(summed, 1)
                    pool.wait_ge(summed, i * (CHUNKS + 2) + (q + 3))
                    pool.sem_inc(direct_free, 1)
                    if q == 0 and not last:
                        gather(FIELDS // 2, FIELDS)
                pool.tensor_tensor(half[:, :, :], total[:, :, 0:N // 2], total[:, :, N // 2:N], ALU.add).then_inc(summed, 1)
                pool.wait_ge(summed, i * (CHUNKS + 2) + (CHUNKS + 3))
                pool.tensor_tensor(logits[:, :, bass.ds(i * BLOCK, BLOCK)], half[:, :, 0:BLOCK], half[:, :, BLOCK:2 * BLOCK], ALU.add).then_inc(summed, 1)

            pool.sem_inc(summed, 2)
            with pool.Fori(0, BLOCKS - 1) as i:
                body(i, False)
            body(BLOCKS - 1, True)
            pool.wait_ge(summed, BLOCKS * (CHUNKS + 2) + 2)
            pool.sem_inc(logits_ready, 1)

        @block.scalar
        def _(act):
            for layer in range(3):
                act.dma_start(bias[:, layer:layer + 1], A[f"L0_rec_b{layer}"].rearrange("(s a) -> s a", a=1)).then_inc(small_in, 16)
            act.dma_start(dense[:, :, :], A["dense_ctx"].rearrange("(j p) c -> p j c", p=BLOCK)).then_inc(small_in, 16)
            with nc.allow_non_contiguous_dma(reason="small columns"):
                act.dma_start(wt3[:, :], A["W_top3"].rearrange("(t p) n -> p (t n)", p=PART)).then_inc(top_in, 16)
                act.dma_start(bt1[:, :], A["b_top1"].rearrange("(t p) -> p t", p=PART)).then_inc(top_in, 16)
                act.dma_start(bt2[:, :], A["b_top2"].rearrange("(t p) -> p t", p=PART)).then_inc(top_in, 16)

            def store_block(i):
                act.wait_ge(transposed, i + 1)
                act.activation(xt[:, 0:4, :].rearrange("p t n -> p (t n)"), tp[0][:, :], ACT.Copy).then_inc(xt_ready, 1)
                act.activation(xt[0:FIELDS * DIM - 4 * PART, 4, :], tp[1][0:FIELDS * DIM - 4 * PART, 0:BLOCK], ACT.Copy).then_inc(xt_ready, 1)
                act.wait_ge(xt_ready, i * 2 + 2)
                at = i * FBLOCK
                tail = FIELDS * DIM - 4 * PART
                act.dma_start(bass.AP(fields.tensor, at, [[BLOCK, PART], [PART * BLOCK, 4], [1, BLOCK]]), xt[:, 0:4, :]).then_inc(stored, 16)
                act.dma_start(bass.AP(fields.tensor, at + 4 * PART * BLOCK, [[BLOCK, tail], [1, BLOCK]]), xt[0:tail, 4, :]).then_inc(stored, 16)
                wrap = at + FIELDS * DIM * BLOCK
                left = WRAP * DIM - 2 * PART
                act.dma_start(bass.AP(fields.tensor, wrap, [[BLOCK, PART], [PART * BLOCK, 2], [1, BLOCK]]), xt[:, 0:2, :]).then_inc(stored, 16)
                act.dma_start(bass.AP(fields.tensor, wrap + 2 * PART * BLOCK, [[BLOCK, left], [1, BLOCK]]), xt[0:left, 2, :]).then_inc(stored, 16)

            def kept(layer):
                act.activation(xk[layer][0:KEEP, :], z[layer][0:KEEP, :], RELU, bias=bias[0:KEEP, layer:layer + 1]).then_inc(x_ready[layer], 1)
                act.activation(xk[layer][KEEP:OUT, :], z[layer][0:KEEP, :], RELU, bias=bias[0:KEEP, layer:layer + 1]).then_inc(x_ready[layer], 1)

            def layer0_out(c, b):
                act.wait_ge(whole_free, whole_at(c, 0, G0 - 1) + (1 + WHOLE_SLOTS))
                act.wait_ge(stack_ready, c * 2 + 3)
                kept(0)
                act.wait_ge(direct_free, c + 2)
                act.activation(direct[b][0:KEEP, 0, :], z[0][KEEP:OUT, :], RELU, bias=bias[KEEP:OUT, 0:1]).then_inc(z_read[0], 1)

            def layer1_out(c, b):
                act.wait_ge(stack_free, c * 2 + 2)
                act.wait_ge(stack_ready, c * 2 + 2)
                kept(1)
                act.activation(direct[b][KEEP:OUT, 0, :], z[1][KEEP:OUT, :], RELU, bias=bias[KEEP:OUT, 1:2]).then_inc(z_read[1], 1)

            def layer2_out(c, b):
                act.wait_ge(stack_free, c * 2 + 3)
                act.activation(direct[b][:, 1, :], z[2][:, :], RELU, bias=bias[:, 2:3]).then_inc(z_read[2], 1)

            def high_part(i, q, n):
                c = i * CHUNKS + q
                k = q * SPLIT_CHUNK + n
                act.wait_ge(raw_ready, c * SPLIT_CHUNK + (n + 1))
                act.wait_ge(parts_free, c * SPLIT_CHUNK + (n + 1))
                act.activation(high[:, k % PART_SLOTS], raw[:, k % RAW_SLOTS], ACT.Copy).then_inc(high_ready, 1)

            def stack_part(c, n):
                act.wait_ge(stack_ready, c * 2 + (n + 3))
                act.wait_ge(stack_free, c * 2 + (n + 1))
                act.activation(stack[:, :], stack_raw[:, :], ACT.Copy).then_inc(stack_high, 1)

            S1 = len(SPLIT[1])

            def body(i, last):
                for q in range(CHUNKS):
                    c = i * CHUNKS + q
                    final = last and q == CHUNKS - 1
                    for n in range(HEAD, S1):
                        high_part(i, q, n)
                    stack_part(c, 0)
                    layer1_out(c, q % 2)
                    for n in range(S1, S1 + HEAD2):
                        high_part(i, q, n)
                    if not final:
                        layer0_out(c, (q + 1) % 2)
                    if q == 2 and not last:
                        store_block(i + 1)
                    for n in range(S1 + HEAD2, SPLIT_CHUNK):
                        high_part(i, q, n)
                    stack_part(c, 1)
                    if not final:
                        for n in range(HEAD):
                            high_part(i, q + 1, n)
                    layer2_out(c, q % 2)

            act.wait_ge(small_in, 64)
            store_block(0)
            act.wait_ge(dense_t, 1)
            act.activation(denseT[:, :], top[0:DENSE, :], ACT.Copy).then_inc(dense_ready, 1)
            act.wait_ge(w12_in, 96)
            for n, w, t in split_weights:
                act.activation(w_high[:, n, :], w[:, t, :], ACT.Copy).then_inc(w_split, 1)
            act.wait_ge(whole_free, G0 + WHOLE_SLOTS)
            kept(0)
            act.wait_ge(direct_free, 1)
            act.activation(direct[0][0:KEEP, 0, :], z[0][KEEP:OUT, :], RELU, bias=bias[KEEP:OUT, 0:1]).then_inc(z_read[0], 1)
            for n in range(HEAD):
                high_part(0, 0, n)
            with act.Fori(0, BLOCKS - 1) as i:
                body(i, False)
            body(BLOCKS - 1, True)

            act.wait_ge(top_in, 16 * 6)
            act.wait_ge(whole_free, BLOCKS * CHUNKS * WHOLE_CHUNK + WHOLE_SLOTS)
            for m in range(H1 // PART):
                act.wait_ge(h1_done, m + 1)
                act.activation(h1[:, m, :], (top, tp[0], tp[1], z[0])[m][:, :], RELU, bias=bt1[:, m:m + 1]).then_inc(h1_ready, 1)
            for m in range(H2 // PART):
                act.wait_ge(h2_done, m + 1)
                act.activation(h2[:, m, :], (z[1], z[2])[m][:, :], RELU, bias=bt2[:, m:m + 1]).then_inc(h2_ready, 1)
            act.wait_ge(y_done, 1)
            act.activation(y, xk[0][0:1, :], ACT.Copy).then_inc(y_ready, 1)

        @block.vector
        def _(dve):
            dve.wait_ge(w0_in, 64)
            nc.vector.tensor_tensor(w0[0:ROWS0, 0:T0 - 1, :], w0[0:ROWS0, 0:T0 - 1, :], w0_rev[0:ROWS0, 0:T0 - 1, :], ALU.add).then_inc(w0_ready, 1)
            nc.vector.tensor_tensor(w0[0:LAST0, T0 - 1, :], w0[0:LAST0, T0 - 1, :], w0_rev[0:LAST0, T0 - 1, :], ALU.add).then_inc(w0_ready, 1)
            dve.sem_inc(whole_free, WHOLE_SLOTS)
            dve.sem_inc(low_ready, RAW_SLOTS)
            dve.sem_inc(parts_free, PART_SLOTS)
            dve.sem_inc(stack_ready, 2)
            dve.sem_inc(stack_low, 1)
            dve.sem_inc(stack_free, 1)
            dve.sem_inc(bc_free, SECTIONS)
            dve.sem_inc(direct_free, 2)
            dve.wait_ge(w12_in, 96)
            dve.wait_ge(w_split, len(split_weights))
            for n, w, t in split_weights:
                nc.vector.tensor_tensor(w_low[:, n, :], w[:, t, :], w_high[:, n, :], ALU.subtract).then_inc(w_split, 1)
            dve.wait_ge(w0_ready, 2)

            def layer0_products(count, k0, fills):
                dve.wait_ge(rot_in, fills * 96)
                for g in range(G0):
                    dve.wait_ge(whole_free, count + (g + 1))
                    slot = (k0 + g) % WHOLE_SLOTS
                    if g < G0 - 1:
                        ins = nc.vector.tensor_tensor(whole[0:ROWS0, slot], rot[:, GT * g:GT * g + GT, :],
                                                      rep[:, None, :].to_broadcast([ROWS0, GT, N]), ALU.mult)
                    else:
                        ins = nc.vector.tensor_tensor(whole[0:LAST0, slot, 0], rot[0:LAST0, T0 - 1, :], rep[0:LAST0, :], ALU.mult)
                    ins.then_inc(whole_ready, 1)

            def low_part(i, q, n):
                c = i * CHUNKS + q
                k = q * SPLIT_CHUNK + n
                dve.wait_ge(high_ready, c * SPLIT_CHUNK + (n + 1))
                nc.vector.tensor_tensor(low[:, k % PART_SLOTS], raw[:, k % RAW_SLOTS], high[:, k % PART_SLOTS], ALU.subtract).then_inc(low_ready, 1)

            def field_products(i, q, layer, final, hook):
                c = i * CHUNKS + q
                pending = []
                x = xk[layer - 1]
                dve.wait_ge(x_ready[layer - 1], c * 2 + 2)
                for g in range(G1):
                    if layer == 1 and g % (SECTION // GT) == 0:
                        n = g // (SECTION // GT)
                        dve.wait_ge(bc_in[n], (c + 1) * (32 if n < SECTIONS - 1 else 48))
                    if is_split(layer, g):
                        n = number(layer, g, final)
                        k = q * SPLIT_CHUNK + n
                        dve.wait_ge(low_ready, c * SPLIT_CHUNK + (n + 1))
                        nc.vector.tensor_tensor(raw[:, k % RAW_SLOTS], bc[:, GT * g:GT * g + GT, :],
                                                x[:, None, :].to_broadcast([PART, GT, N]), ALU.mult).then_inc(raw_ready, 1)
                        pending.append((g, n))
                    else:
                        count = whole_at(c, layer, g, final)
                        dve.wait_ge(whole_free, count + 1)
                        slot = whole_at(q, layer, g, final) % WHOLE_SLOTS
                        if g < G1 - 1:
                            ins = nc.vector.tensor_tensor(whole[:, slot], bc[:, GT * g:GT * g + GT, :],
                                                          x[:, None, :].to_broadcast([PART, GT, N]), ALU.mult)
                        else:
                            ins = nc.vector.tensor_tensor(whole[:, slot, 0], bc[:, T1 - 2, :], x[:, :], ALU.mult)
                        ins.then_inc(whole_ready, 1)
                    if g == 0:
                        hook()
                    if pending and g - pending[0][0] >= LAG:
                        low_part(i, q, pending.pop(0)[1])
                    if layer == 2 and g and g % (SECTION // GT) == 0:
                        release(c, g - 1, final)
                dve.wait_ge(stack_low, c * 2 + layer)
                nc.vector.tensor_tensor(stack_raw[:, :], bc[:, T1 - 1, :], x[:, :], ALU.mult).then_inc(stack_ready, 1)
                for _, n in pending:
                    low_part(i, q, n)
                dve.wait_ge(stack_high, c * 2 + layer)
                nc.vector.tensor_tensor(stack[KEEP:PART, :], stack_raw[KEEP:PART, :], stack[KEEP:PART, :], ALU.subtract).then_inc(stack_low, 1)
                if layer == 2:
                    dve.wait_ge(stack_ready, c * 2 + 4)
                    dve.sem_inc(bc_free, 1)

            def release(c, g, final):
                for h in (g - 1, g):
                    if h < g and is_split(2, h) == is_split(2, g):
                        continue
                    if is_split(2, h):
                        dve.wait_ge(raw_ready, split_at(c, 2, h) + 1)
                    else:
                        dve.wait_ge(whole_ready, whole_at(c, 2, h, final) + 1)
                dve.sem_inc(bc_free, 1)

            def body(i, last):
                for q in range(CHUNKS):
                    c = i * CHUNKS + q
                    final = last and q == CHUNKS - 1
                    field_products(i, q, 1, final, lambda: None)

                    def rotations_read():
                        dve.wait_ge(whole_ready, whole_at(c, 0, G0 - 1) + 1)
                        dve.sem_inc(rot_free, 1)

                    if not final:
                        layer0_products(whole_at(c, 0, 0), whole_at(q, 0, 0), c + 2)
                    field_products(i, q, 2, final, (lambda: None) if final else rotations_read)

            layer0_products(0, 0, 1)
            dve.wait_ge(whole_ready, G0)
            dve.sem_inc(rot_free, 1)
            with dve.Fori(0, BLOCKS - 1) as i:
                body(i, False)
            body(BLOCKS - 1, True)

        @block.tensor
        def _(pe):
            def transposes(i, first=False):
                pe.wait_ge(gathered, (i + 1) * (16 * FIELDS))
                if not first:
                    pe.wait_ge(xt_ready, i * 2)
                for t in range(TSLICES):
                    m = min(PART, FIELDS * DIM - t * PART)
                    dst = tp[0][0:m, t * BLOCK:(t + 1) * BLOCK] if t < 4 else tp[1][0:m, 0:BLOCK]
                    ins = nc.tensor.transpose(dst, rows[:, t * PART:t * PART + m], ident[:, :])
                ins.then_inc(transposed, 1)

            def layer0(count, k0, c):
                pe.wait_ge(z_read[0], c + 1)
                for g in range(G0):
                    slot = (k0 + g) % WHOLE_SLOTS
                    pe.wait_ge(whole_ready, count + (g + 1))
                    for t in range(GT * g, min(T0, GT * g + GT)):
                        k = ROWS0 if t < T0 - 1 else LAST0
                        ins = nc.tensor.matmul(z[0][:, :], w0[0:k, t, :], whole[0:k, slot, t - GT * g], start=(t == 0), stop=(t == T0 - 1))
                    ins.then_inc(whole_free, 1)

            def fields_layer(i, q, layer, w, final):
                c = i * CHUNKS + q
                out_z = z[layer][:, :]
                pe.wait_ge(z_read[layer], c + 1)
                for g in range(G1):
                    if is_split(layer, g):
                        n = number(layer, g, final)
                        k = (q * SPLIT_CHUNK + n) % PART_SLOTS
                        pe.wait_ge(low_ready, c * SPLIT_CHUNK + (n + 1 + RAW_SLOTS))
                        for u in range(GT):
                            nc.tensor.matmul(out_z, w_high[:, GT * n + u, :], high[:, k, u], start=(g == 0 and u == 0), stop=False)
                            nc.tensor.matmul(out_z, w_low[:, GT * n + u, :], high[:, k, u], start=False, stop=False)
                            ins = nc.tensor.matmul(out_z, w_high[:, GT * n + u, :], low[:, k, u], start=False, stop=False)
                        ins.then_inc(parts_free, 1)
                    else:
                        pe.wait_ge(whole_ready, whole_at(c, layer, g, final) + 1)
                        slot = whole_at(q, layer, g, final) % WHOLE_SLOTS
                        for t in range(GT * g, min(T1 - 1, GT * g + GT)):
                            ins = nc.tensor.matmul(out_z, w[:, t, :], whole[:, slot, t - GT * g], start=(t == 0), stop=False)
                        ins.then_inc(whole_free, 1)
                n = GT * SPLIT_CHUNK + layer - 1
                pe.wait_ge(stack_low, c * 2 + (layer + 1))
                nc.tensor.matmul(out_z, w_high[:, n, :], stack[:, :], start=False, stop=False)
                nc.tensor.matmul(out_z, w_low[:, n, :], stack[:, :], start=False, stop=True).then_inc(stack_free, 1)

            def body(i, last):
                for q in range(CHUNKS):
                    c = i * CHUNKS + q
                    final = last and q == CHUNKS - 1
                    fields_layer(i, q, 1, w1, final)
                    if not final:
                        layer0(whole_at(c, 0, 0), whole_at(q, 0, 0), c + 1)
                    if q == 2 and not last:
                        transposes(i + 1)
                    fields_layer(i, q, 2, w2, final)

            for layer in range(3):
                pe.sem_inc(z_read[layer], 1)
            pe.wait_ge(ident_ready, 1)
            pe.wait_ge(small_in, 64)
            for j in range(BLOCKS):
                ins = nc.tensor.transpose(top[0:DENSE, j * BLOCK:(j + 1) * BLOCK], dense[:, j, :], ident[:, :])
            ins.then_inc(dense_t, 1)
            transposes(0, first=True)
            pe.wait_ge(w0_ready, 2)
            layer0(0, 0, 0)
            pe.wait_ge(w12_in, 96)
            pe.wait_ge(w_split, 2 * len(split_weights))
            with pe.Fori(0, BLOCKS - 1) as i:
                body(i, False)
            body(BLOCKS - 1, True)

            pe.wait_ge(top_in, 16 * 6)
            pe.wait_ge(dense_ready, 1)
            pe.wait_ge(logits_ready, 1)
            pe.wait_ge(xt_ready, 2 * BLOCKS)
            pe.wait_ge(z_read[0], BLOCKS * CHUNKS + 1)
            for m in range(H1 // PART):
                dst = (top, tp[0], tp[1], z[0])[m]
                for t in range(2):
                    nc.tensor.matmul(dst[:, :], wt1[:, t, m * PART:(m + 1) * PART], logits[:, t, :], start=(t == 0), stop=False)
                nc.tensor.matmul(dst[:, :], wt1_dense[:, m * PART:(m + 1) * PART], denseT[:, :], start=False, stop=True).then_inc(h1_done, 1)
            pe.wait_ge(h1_ready, H1 // PART)
            for layer in (1, 2):
                pe.wait_ge(z_read[layer], BLOCKS * CHUNKS + 1)
            for m in range(H2 // PART):
                for t in range(H1 // PART):
                    ins = nc.tensor.matmul((z[1], z[2])[m][:, :], wt2[:, t, m * PART:(m + 1) * PART], h1[:, t, :], start=(t == 0), stop=(t == H1 // PART - 1))
                ins.then_inc(h2_done, 1)
            pe.wait_ge(h2_ready, H2 // PART)
            pe.wait_ge(stack_ready, BLOCKS * CHUNKS * 2 + 2)
            for t in range(H2 // PART):
                ins = nc.tensor.matmul(xk[0][0:1, :], wt3[:, t:t + 1], h2[:, t, :], start=(t == 0), stop=(t == H2 // PART - 1))
            ins.then_inc(y_done, 1)


def kernel(**inputs):
    import numpy as _np
    import concourse.bacc as _bacc
    from concourse import mybir as _mybir
    from concourse.bass_utils import run_bass_kernel_spmd as _run

    nc = _bacc.Bacc("TRN2", target_bir_lowering=False, num_devices=1)
    given = {k: _np.ascontiguousarray(v) for k, v in inputs.items() if k != "L0_rec_w0"}
    w0 = _np.asarray(inputs["L0_rec_w0"])
    r, i = _np.arange(ROT)[:, None], _np.arange(FIELDS)[None, :]
    j = (i + r) % FIELDS
    given["w0_fwd"] = _np.ascontiguousarray(w0[i + 0 * r, j].reshape(ROT * FIELDS, OUT))
    rev = w0[j, i + 0 * r].reshape(ROT * FIELDS, OUT).copy()
    rev[0:FIELDS] = 0
    given["w0_rev"] = rev
    arrays, aps = {}, {}
    for name, a in given.items():
        arrays["in_" + name] = a
        aps[name] = nc.dram_tensor("in_" + name, a.shape, _mybir.dt.from_np(a.dtype), kind="ExternalInput").ap()
    fields = nc.dram_tensor("fields", (BLOCKS * XROWS * BLOCK,), _mybir.dt.float32).ap()
    out = nc.dram_tensor("out_y", (BATCH, 1), _mybir.dt.float32, kind="ExternalOutput").ap()
    tower(nc, aps, fields, out)
    result = _run(nc, [arrays], core_ids=[0])
    return result.results[0]["out_y"]
```

```python
import concourse.bass as bass
from concourse import mybir
from contextlib import ExitStack

BATCH, FIELDS, DIM = 512, 39, 16
PART = 128
OUT = 128
KEEP = OUT // 2
SUB = 32
N = DIM * SUB
CHUNKS = BATCH // SUB
BODY = 4
LOOPS = CHUNKS // BODY
BY = PART // SUB
GATHERS = -(-FIELDS // BY)
ROT = FIELDS // 2 + 1
ROT_PER_TILE = PART // FIELDS
T0 = -(-ROT // ROT_PER_TILE)
ROWS0 = ROT_PER_TILE * FIELDS
LAST0 = (ROT - (T0 - 1) * ROT_PER_TILE) * FIELDS
T1 = -(-FIELDS // 2)
WRAP = 2 * GATHERS
GT = 2
G0 = -(-T0 // GT)
G1 = T1 // GT
SPLIT = {0: (1,), 1: (2, 4, 6, 8), 2: (2, 5, 8)}
WHOLE_CHUNK = G0 + 2 * G1 - sum(map(len, SPLIT.values()))
SPLIT_CHUNK = sum(map(len, SPLIT.values()))
WHOLE_SLOTS = 4
RAW_SLOTS = 2
PART_SLOTS = 4
LAG = 2
SECTION = 4
SECTIONS = T1 // SECTION
STORES = 5
H1, H2, DENSE = 512, 256, 16


def tower(nc, A, fields, out):
    fp32, fp32r, i32 = mybir.dt.float32, mybir.dt.float32r, mybir.dt.int32
    ALU, ACT = mybir.AluOpType, mybir.ActivationFunctionType
    RELU = ACT.Relu

    with ExitStack() as ctx:
        def sb(name, shape, dt=fp32):
            return ctx.enter_context(nc.sbuf_tensor(name, shape, dt))

        def bank(name):
            return ctx.enter_context(nc.psum_tensor(name, [PART, N], fp32))

        def sem(name):
            return ctx.enter_context(nc.semaphore(name))

        w0 = sb("w0", [PART, T0, OUT])
        w1 = sb("w1", [PART, T1, OUT])
        w2 = sb("w2", [PART, T1, OUT])
        w_high = sb("w_high", [PART, GT * SPLIT_CHUNK + 2, OUT], fp32r)
        w_low = sb("w_low", [PART, GT * SPLIT_CHUNK + 2, OUT], fp32r)
        wt3 = sb("wt3", [PART, H2 // PART])
        bias = sb("bias", [PART, 3])
        bt1 = sb("bt1", [PART, H1 // PART])
        bt2 = sb("bt2", [PART, H2 // PART])
        ident = sb("ident", [PART, PART])
        ids_all = sb("ids_all", [PART, CHUNKS, GATHERS], i32)
        base = sb("base", [PART, GATHERS], i32)
        rows_all = sb("rows_all", [PART, CHUNKS, GATHERS], i32)
        idx = sb("idx", [PART, GATHERS], i32)
        emb = sb("emb", [PART, GATHERS * DIM])
        xt = sb("xt", [PART, 2, PART])
        rot = sb("rot", [ROWS0, T0, N])
        rep = sb("rep", [ROWS0, N])
        bc = sb("bc", [PART, T1, N])
        whole = sb("whole", [PART, WHOLE_SLOTS, GT, N])
        raw = sb("raw", [PART, RAW_SLOTS, GT, N])
        high = sb("high", [PART, PART_SLOTS, GT, N], fp32r)
        low = sb("low", [PART, PART_SLOTS, GT, N], fp32r)
        stack_raw = sb("stack_raw", [PART, N])
        stack = sb("stack", [PART, N], fp32r)
        direct = [sb(f"direct{n}", [PART, 2, N]) for n in range(2)]
        halves = [sb(f"sum{n}", [PART, 2, n * SUB]) for n in (8, 4, 2)]
        logits = sb("logits", [PART, 2, BATCH])
        dense = sb("dense", [PART, BATCH // PART, DENSE])
        denseT = sb("denseT", [DENSE, BATCH])
        w0_rev = whole[:, 0:2].rearrange("p a b n -> p (a b n)")[:, 0:T0 * OUT].rearrange("p (t s) -> p t s", s=OUT)
        wt1 = bc[:, 0:2, :]
        wt1_dense = bc[0:DENSE, 2, :]
        wt2 = bc[:, 3:5, :].rearrange("p a (b n) -> p (a b) n", n=H2)
        h1 = whole[:, 0:2].rearrange("p a b n -> p (a b) n")
        h2 = whole[:, 2]
        y = whole[0:1, 3, 0]

        z = [bank(f"z{n}") for n in range(3)]
        xk = [bank(f"xk{n}") for n in range(2)]
        tp = bank("tp")
        top = [bank(f"top{n}") for n in range(2)]
        h1_banks = (top[0], top[1], tp, z[0])

        ids_in = sem("ids_in")
        w0_in = sem("w0_in")
        w12_in = sem("w12_in")
        small_in = sem("small_in")
        top_in = sem("top_in")
        ident_zero = sem("ident_zero")
        ident_ready = sem("ident_ready")
        w0_ready = sem("w0_ready")
        idx_ready = sem("idx_ready")
        gathered = sem("gathered")
        transposed = sem("transposed")
        xt_ready = sem("xt_ready")
        stored = sem("stored")
        rot_free = sem("rot_free")
        bc_free = sem("bc_free")
        rot_first = sem("rot_first")
        rot_rest = sem("rot_rest")
        bc_in = [sem(f"bc_in{n}") for n in range(SECTIONS)]
        whole_ready = sem("whole_ready")
        whole_free = sem("whole_free")
        raw_ready = sem("raw_ready")
        high_ready = sem("high_ready")
        low_ready = sem("low_ready")
        parts_free = sem("parts_free")
        stack_ready = sem("stack_ready")
        stack_high = sem("stack_high")
        stack_low = sem("stack_low")
        stack_free = sem("stack_free")
        w_split = sem("w_split")
        sp_step = sem("sp_step")
        z_read = [sem(f"z_read{n}") for n in range(3)]
        x_ready = [sem(f"x_ready{n}") for n in range(2)]
        direct_free = sem("direct_free")
        summed = sem("summed")
        dense_t = sem("dense_t")
        dense_ready = sem("dense_ready")
        h1_done = sem("h1_done")
        h1_ready = sem("h1_ready")
        h2_done = sem("h2_done")
        h2_ready = sem("h2_ready")
        y_done = sem("y_done")
        y_ready = sem("y_ready")
        written = sem("written")
        pool_step = sem("pool_step")

        block = ctx.enter_context(nc.Block())

        CHUNK_ROWS = (FIELDS + WRAP) * N

        STEP = [(1, g) for g in range(G1)] + [(0, g) for g in range(G0)] + [(2, g) for g in range(G1)]

        def is_split(layer, g):
            return g in SPLIT[layer]

        def number(layer, g, final):
            kind = is_split(layer, g)
            n = sum(is_split(*x) == kind for x in STEP[:STEP.index((layer, g))])
            first = sum(is_split(0, h) == kind for h in range(G0))
            return n + (0 if final and layer == 2 else first)

        def whole_at(c, layer, g, final=False):
            return c * WHOLE_CHUNK + number(layer, g, final)

        def split_at(c, layer, g, final=False):
            return c * SPLIT_CHUNK + number(layer, g, final)

        S0 = len(SPLIT[0])
        SPLIT_GROUPS = [x for x in STEP if is_split(*x)]
        PARTS_AT = {x: GT * n for n, x in enumerate(SPLIT_GROUPS)}
        FIRST_WHOLE = next(g for g in range(G0) if not is_split(0, g))

        def split_before(c):
            return c * SPLIT_CHUNK + (S0 + len(SPLIT[1]))

        ROWS = (ROWS0, PART, PART)
        HEAD = 1
        AHEAD = 6
        HEAD2 = 1
        split_weights = [(GT * n + u, (w0, w1, w2)[layer], GT * g + u)
                         for n, (layer, g) in enumerate(SPLIT_GROUPS) for u in range(GT)]
        split_weights += [(GT * SPLIT_CHUNK + n, w, T1 - 1) for n, w in enumerate((w1, w2))]

        @block.sync
        def _(sp):
            sp.dma_start(ids_all[:, :, :], A["ids"]).then_inc(ids_in, 16)
            sp.dma_start(base[:, :], A["base"]).then_inc(ids_in, 16)
            full = (T0 - 1) * ROWS0
            for src, dst in ((A["w0_fwd"], w0), (A["w0_rev"], w0_rev)):
                sp.dma_start(dst[0:ROWS0, 0:T0 - 1, :], src[0:full, :].rearrange("(t p) s -> p t s", p=ROWS0)).then_inc(w0_in, 16)
                sp.dma_start(dst[0:LAST0, T0 - 1, :], src[full:full + LAST0, :]).then_inc(w0_in, 16)
            for name, dst in (("L0_rec_w1", w1), ("L0_rec_w2", w2)):
                flat = A[name].rearrange("h k s -> (h k) s")
                body = (T1 - 1) * PART
                sp.dma_start(dst[:, 0:T1 - 1, :], flat[0:body, :].rearrange("(t p) s -> p t s", p=PART)).then_inc(w12_in, 16)
                for part in range(2):
                    sp.dma_start(dst[part * KEEP:(part + 1) * KEEP, T1 - 1, :], flat[body:body + KEEP, :]).then_inc(w12_in, 16)

            def load_rotations(at):
                for r in range(ROT_PER_TILE):
                    src = bass.AP(fields.tensor, at, [[N, FIELDS], [1, N]])
                    sp.dma_start(rep[r * FIELDS:(r + 1) * FIELDS, :], src).then_inc(rot_first, 16)
                for first, last, arrived in ((0, GT, rot_first), (GT, T0, rot_rest)):
                    for r in range(ROT_PER_TILE):
                        tiles = len(range(r + first * ROT_PER_TILE, min(ROT, last * ROT_PER_TILE), ROT_PER_TILE))
                        src = bass.AP(fields.tensor, at + (first * ROT_PER_TILE + r) * N, [[N, FIELDS], [ROT_PER_TILE * N, tiles], [1, N]])
                        sp.dma_start(rot[r * FIELDS:(r + 1) * FIELDS, first:first + tiles, :], src).then_inc(arrived, 16)

            def load_broadcasts(at, c):
                for n in range(SECTIONS):
                    sp.wait_ge(bc_free, c * SECTIONS + (n + 1))
                    for parity in range(2):
                        first = 2 * SECTION * n + parity
                        tiles = len(range(first, min(FIELDS, 2 * SECTION * (n + 1)), 2))
                        src = bass.AP(fields.tensor, at + first * N, [[0, KEEP], [2 * N, tiles], [1, N]])
                        sp.dma_start(bc[parity * KEEP:(parity + 1) * KEEP, SECTION * n:SECTION * n + tiles, :], src).then_inc(bc_in[n], 16)
                src = bass.AP(fields.tensor, at + (FIELDS - 1) * N, [[0, KEEP], [1, N]])
                sp.dma_start(bc[KEEP:PART, T1 - 1, :], src).then_inc(bc_in[SECTIONS - 1], 16)

            def body(i, last):
                for q in range(BODY):
                    c = i * BODY + q
                    load_broadcasts((i * BODY + q) * CHUNK_ROWS, c)
                    if q < BODY - 1 or not last:
                        sp.wait_ge(stored, (c + 2) * (16 * STORES))
                        sp.sem_inc(sp_step, 1)
                        sp.wait_ge(rot_free, c + 1)
                        sp.sem_inc(sp_step, 1)
                        load_rotations((c + 1) * CHUNK_ROWS)

            sp.wait_ge(stored, 16 * STORES)
            load_rotations(0)
            with sp.Fori(0, LOOPS - 1) as i:
                body(i, False)
            body(LOOPS - 1, True)
            sp.wait_ge(bc_free, (CHUNKS + 1) * SECTIONS)
            sp.dma_start(wt1[:, :, :], A["W_top1"][0:2 * OUT, :].rearrange("(t p) n -> p t n", p=PART)).then_inc(top_in, 16)
            sp.dma_start(wt1_dense[:, :], A["W_top1"][2 * OUT:2 * OUT + DENSE, :]).then_inc(top_in, 16)
            sp.dma_start(wt2[:, :, :], A["W_top2"].rearrange("(t p) n -> p t n", p=PART)).then_inc(top_in, 16)
            sp.wait_ge(y_ready, 1)
            sp.dma_start(out.rearrange("(a b) c -> a (b c)", a=1), y).then_inc(written, 16)
            sp.wait_ge(written, 16)

        @block.gpsimd
        def _(pool):
            pool.memset(ident[:, :], 0.0).then_inc(ident_zero, 1)
            pool.wait_ge(ident_zero, 1)
            pool.affine_select(out=ident[:, :], in_=ident[:, :], compare_op=ALU.not_equal, fill=1.0,
                               base=0, pattern=[[-1, PART]], channel_multiplier=1).then_inc(ident_ready, 1)
            pool.wait_ge(ids_in, 32)

            pool.tensor_tensor(rows_all[:, :, :], ids_all[:, :, :], base[:, None, :].to_broadcast([PART, CHUNKS, GATHERS]), ALU.add).then_inc(idx_ready, 1)

            def gather():
                for j in range(GATHERS):
                    pool.indirect_dma_start(emb[:, j * DIM:(j + 1) * DIM], None, A["tables"],
                                            bass.IndirectOffsetOnAxis(idx[:, j:j + 1], 0)).then_inc(gathered, 16)

            for c in range(2):
                pool.wait_ge(idx_ready, c + 1)
                if c:
                    pool.wait_ge(transposed, c)
                pool.tensor_copy(idx[:, :], rows_all[:, c, :]).then_inc(idx_ready, 1)
                pool.wait_ge(idx_ready, c + 2)
                gather()

            def body(i, last):
                def stack_part(c, q, n):
                    pool.wait_ge(stack_high, c * 2 + (n + 1))
                    pool.wait_ge(summed, c * 4 + 1)
                    pool.wait_ge(gathered, CHUNKS * 16 * GATHERS if last and q + n >= BODY - 2 else (c + (n + 2)) * (16 * GATHERS))
                    pool.tensor_tensor(stack[KEEP:PART, :], stack_raw[KEEP:PART, :], stack[KEEP:PART, :], ALU.subtract).then_inc(stack_low, 1)
                    pool.wait_ge(stack_low, c * 2 + (n + 2))
                    pool.sem_inc(pool_step, 1)

                for q in range(BODY):
                    c = i * BODY + q
                    stack_part(c, q, 0)
                    if not (last and q >= BODY - 2):
                        pool.wait_ge(transposed, c + 2)
                        pool.sem_inc(pool_step, 1)
                        pool.tensor_copy(idx[:, :], rows_all[:, c + 2, :]).then_inc(idx_ready, 1)
                        pool.wait_ge(idx_ready, c + 4)
                        pool.sem_inc(pool_step, 1)
                        gather()
                    stack_part(c, q, 1)
                    for layer in range(3):
                        pool.wait_ge(z_read[layer], c + 2)
                    src = direct[q % 2]
                    width = DIM
                    for n, dst in enumerate(halves + [logits[:, :, bass.ds(c * SUB, SUB)]]):
                        width //= 2
                        pool.wait_ge(summed, c * 4 + (n + 1))
                        if n == 1:
                            pool.sem_inc(direct_free, 1)
                        dst = dst[:, :, :]
                        pool.tensor_tensor(dst, src[:, :, 0:width * SUB], src[:, :, width * SUB:2 * width * SUB], ALU.add).then_inc(summed, 1)
                        src = dst

            pool.sem_inc(summed, 1)
            with pool.Fori(0, LOOPS - 1) as i:
                body(i, False)
            body(LOOPS - 1, True)

        @block.scalar
        def _(act):
            for layer in range(3):
                act.dma_start(bias[:, layer:layer + 1], A[f"L0_rec_b{layer}"].rearrange("(s a) -> s a", a=1)).then_inc(small_in, 16)
            act.dma_start(dense[:, :, :], A["dense_ctx"].rearrange("(j p) c -> p j c", p=PART)).then_inc(small_in, 16)
            with nc.allow_non_contiguous_dma(reason="small columns"):
                act.dma_start(wt3[:, :], A["W_top3"].rearrange("(t p) n -> p (t n)", p=PART)).then_inc(top_in, 16)
                act.dma_start(bt1[:, :], A["b_top1"].rearrange("(t p) -> p t", p=PART)).then_inc(top_in, 16)
                act.dma_start(bt2[:, :], A["b_top2"].rearrange("(t p) -> p t", p=PART)).then_inc(top_in, 16)

            def store(c, first=False):
                act.wait_ge(transposed, c + 1)
                if not first:
                    act.wait_ge(stored, c * (16 * STORES))
                head = PART // DIM
                rest = (GATHERS - head) * DIM
                act.activation(xt[:, 0, :], tp[:, 0:PART], ACT.Copy).then_inc(xt_ready, 1)
                act.activation(xt[0:rest, 1, :], tp[0:rest, PART:2 * PART], ACT.Copy).then_inc(xt_ready, 1)
                act.wait_ge(xt_ready, c * 2 + 2)
                at = c * CHUNK_ROWS
                turns = GATHERS * N
                for to, parts in ((0, BY), (FIELDS * N, 2)):
                    act.dma_start(bass.AP(fields.tensor, at + to, [[SUB, PART], [turns, parts], [1, SUB]]),
                                  xt[:, 0, 0:parts * SUB].rearrange("p (f b) -> p f b", b=SUB)).then_inc(stored, 16)
                    parts = min(parts, BY - 1)
                    act.dma_start(bass.AP(fields.tensor, at + (to + head * N), [[SUB, rest], [turns, parts], [1, SUB]]),
                                  xt[0:rest, 1, 0:parts * SUB].rearrange("p (f b) -> p f b", b=SUB)).then_inc(stored, 16)
                act.dma_start(bass.AP(fields.tensor, at + (FIELDS - 1) * N, [[SUB, DIM], [1, SUB]]),
                              xt[0:DIM, 1, (BY - 1) * SUB:PART]).then_inc(stored, 16)

            def kept(layer):
                act.activation(xk[layer][0:KEEP, :], z[layer][0:KEEP, :], RELU, bias=bias[0:KEEP, layer:layer + 1]).then_inc(x_ready[layer], 1)
                act.activation(xk[layer][KEEP:OUT, :], z[layer][0:KEEP, :], RELU, bias=bias[0:KEEP, layer:layer + 1]).then_inc(x_ready[layer], 1)

            def layer0_out(c, b):
                act.wait_ge(whole_free, whole_at(c, 0, G0 - 1) + (1 + WHOLE_SLOTS))
                act.wait_ge(stack_ready, c * 2 + 3)
                kept(0)
                act.wait_ge(direct_free, c + 2)
                act.activation(direct[b][0:KEEP, 0, :], z[0][KEEP:OUT, :], RELU, bias=bias[KEEP:OUT, 0:1]).then_inc(z_read[0], 1)

            def layer1_out(c, b):
                act.wait_ge(stack_free, c * 2 + 2)
                act.wait_ge(stack_ready, c * 2 + 2)
                kept(1)
                act.activation(direct[b][KEEP:OUT, 0, :], z[1][KEEP:OUT, :], RELU, bias=bias[KEEP:OUT, 1:2]).then_inc(z_read[1], 1)

            def layer2_out(c, b):
                act.wait_ge(stack_free, c * 2 + 3)
                act.activation(direct[b][:, 1, :], z[2][:, :], RELU, bias=bias[:, 2:3]).then_inc(z_read[2], 1)

            def high_part(count, k, layer):
                act.wait_ge(raw_ready, count + 1)
                act.wait_ge(parts_free, count + 1)
                m = ROWS[layer]
                act.activation(high[0:m, k % PART_SLOTS], raw[0:m, k % RAW_SLOTS], ACT.Copy).then_inc(high_ready, 1)

            def high_group(i, q, layer, g, final):
                high_part(split_at(i * BODY + q, layer, g, final), split_at(q, layer, g, final), layer)

            def stack_part(c, n):
                act.wait_ge(stack_ready, c * 2 + (n + 3))
                act.wait_ge(stack_free, c * 2 + (n + 1))
                act.activation(stack[:, :], stack_raw[:, :], ACT.Copy).then_inc(stack_high, 1)

            def body(i, last):
                for q in range(BODY):
                    c = i * BODY + q
                    final = last and q == BODY - 1
                    for g in SPLIT[1][HEAD:]:
                        high_group(i, q, 1, g, final)
                    stack_part(c, 0)
                    if not final:
                        for g in SPLIT[0]:
                            high_group(i, q, 0, g, final)
                    layer1_out(c, q % 2)
                    for g in SPLIT[2][:HEAD2]:
                        high_group(i, q, 2, g, final)
                    if not final:
                        layer0_out(c, (q + 1) % 2)
                    for g in SPLIT[2][HEAD2:]:
                        high_group(i, q, 2, g, final)
                    stack_part(c, 1)
                    if not (last and q >= BODY - 2):
                        store(c + 2)
                    if not final:
                        for g in SPLIT[1][:HEAD]:
                            high_group(i, q + 1, 1, g, final)
                    layer2_out(c, q % 2)

            act.wait_ge(small_in, 64)
            store(0, first=True)
            act.wait_ge(dense_t, 1)
            act.activation(denseT[:, :], top[0][0:DENSE, :], ACT.Copy).then_inc(dense_ready, 1)
            act.wait_ge(w12_in, 96)
            act.wait_ge(w0_ready, 2)
            for n, w, t in split_weights:
                m = ROWS0 if w is w0 else PART
                act.activation(w_high[0:m, n, :], w[0:m, t, :], ACT.Copy).then_inc(w_split, 1)
            for n in range(S0):
                high_part(n, n, 0)
            act.wait_ge(whole_free, G0 - S0 + WHOLE_SLOTS)
            kept(0)
            act.wait_ge(direct_free, 1)
            act.activation(direct[0][0:KEEP, 0, :], z[0][KEEP:OUT, :], RELU, bias=bias[KEEP:OUT, 0:1]).then_inc(z_read[0], 1)
            for g in SPLIT[1][:HEAD]:
                high_group(0, 0, 1, g, False)
            store(1)
            with act.Fori(0, LOOPS - 1) as i:
                body(i, False)
            body(LOOPS - 1, True)

            act.wait_ge(top_in, 16 * 6)
            act.wait_ge(whole_free, CHUNKS * WHOLE_CHUNK + WHOLE_SLOTS)
            for m in range(H1 // PART):
                act.wait_ge(h1_done, m + 1)
                act.activation(h1[:, m, :], h1_banks[m][:, :], RELU, bias=bt1[:, m:m + 1]).then_inc(h1_ready, 1)
            for m in range(H2 // PART):
                act.wait_ge(h2_done, m + 1)
                act.activation(h2[:, m, :], z[1 + m][:, :], RELU, bias=bt2[:, m:m + 1]).then_inc(h2_ready, 1)
            act.wait_ge(y_done, 1)
            act.activation(y, xk[0][0:1, :], ACT.Copy).then_inc(y_ready, 1)

        @block.vector
        def _(dve):
            dve.wait_ge(w0_in, 64)
            nc.vector.tensor_tensor(w0[0:ROWS0, 0:T0 - 1, :], w0[0:ROWS0, 0:T0 - 1, :], w0_rev[0:ROWS0, 0:T0 - 1, :], ALU.add).then_inc(w0_ready, 1)
            nc.vector.tensor_tensor(w0[0:LAST0, T0 - 1, :], w0[0:LAST0, T0 - 1, :], w0_rev[0:LAST0, T0 - 1, :], ALU.add).then_inc(w0_ready, 1)
            dve.sem_inc(whole_free, WHOLE_SLOTS)
            dve.sem_inc(low_ready, RAW_SLOTS)
            dve.sem_inc(parts_free, PART_SLOTS)
            dve.sem_inc(stack_ready, 2)
            dve.sem_inc(stack_low, 1)
            dve.sem_inc(stack_free, 1)
            dve.sem_inc(bc_free, SECTIONS)
            dve.sem_inc(direct_free, 2)
            dve.wait_ge(w12_in, 96)
            dve.wait_ge(w_split, len(split_weights))
            for n, w, t in split_weights:
                m = ROWS0 if w is w0 else PART
                nc.vector.tensor_tensor(w_low[0:m, n, :], w[0:m, t, :], w_high[0:m, n, :], ALU.subtract).then_inc(w_split, 1)
            dve.wait_ge(w0_ready, 2)

            def layer0_products(whole_count, whole_k, split_count, split_k, fills):
                dve.wait_ge(rot_first, fills * (32 * ROT_PER_TILE))
                w = n = 0
                for g in range(G0):
                    if g == 1:
                        dve.wait_ge(rot_rest, fills * (16 * ROT_PER_TILE))
                    tiles = slice(GT * g, GT * g + GT)
                    twice = rep[:, None, :].to_broadcast([ROWS0, GT, N])
                    if is_split(0, g):
                        dve.wait_ge(low_ready, split_count + (n + 1))
                        nc.vector.tensor_tensor(raw[0:ROWS0, (split_k + n) % RAW_SLOTS], rot[:, tiles, :], twice, ALU.mult).then_inc(raw_ready, 1)
                        n += 1
                        continue
                    dve.wait_ge(whole_free, whole_count + (w + 1))
                    slot = (whole_k + w) % WHOLE_SLOTS
                    w += 1
                    if g < G0 - 1:
                        ins = nc.vector.tensor_tensor(whole[0:ROWS0, slot], rot[:, tiles, :], twice, ALU.mult)
                    else:
                        ins = nc.vector.tensor_tensor(whole[0:LAST0, slot, 0], rot[0:LAST0, T0 - 1, :], rep[0:LAST0, :], ALU.mult)
                    ins.then_inc(whole_ready, 1)
                for n in range(S0):
                    low_part(split_count + n, split_k + n, 0)

            def low_part(count, k, layer):
                m = ROWS[layer]
                dve.wait_ge(high_ready, count + 1)
                nc.vector.tensor_tensor(low[0:m, k % PART_SLOTS], raw[0:m, k % RAW_SLOTS], high[0:m, k % PART_SLOTS], ALU.subtract).then_inc(low_ready, 1)

            def field_products(i, q, layer, final, hook):
                c = i * BODY + q
                pending = []
                x = xk[layer - 1]
                dve.wait_ge(x_ready[layer - 1], c * 2 + 2)
                for g in range(G1):
                    if layer == 1 and g % (SECTION // GT) == 0:
                        n = g // (SECTION // GT)
                        dve.wait_ge(bc_in[n], (c + 1) * (32 if n < SECTIONS - 1 else 48))
                    if is_split(layer, g):
                        k = split_at(q, layer, g, final)
                        dve.wait_ge(low_ready, split_at(c, layer, g, final) + 1)
                        nc.vector.tensor_tensor(raw[:, k % RAW_SLOTS], bc[:, GT * g:GT * g + GT, :],
                                                x[:, None, :].to_broadcast([PART, GT, N]), ALU.mult).then_inc(raw_ready, 1)
                        pending.append(g)
                    else:
                        count = whole_at(c, layer, g, final)
                        dve.wait_ge(whole_free, count + 1)
                        slot = whole_at(q, layer, g, final) % WHOLE_SLOTS
                        if g < G1 - 1:
                            ins = nc.vector.tensor_tensor(whole[:, slot], bc[:, GT * g:GT * g + GT, :],
                                                          x[:, None, :].to_broadcast([PART, GT, N]), ALU.mult)
                        else:
                            ins = nc.vector.tensor_tensor(whole[:, slot, 0], bc[:, T1 - 2, :], x[:, :], ALU.mult)
                        ins.then_inc(whole_ready, 1)
                    if g == 0:
                        hook()
                    if pending and g - pending[0] >= LAG:
                        h = pending.pop(0)
                        low_part(split_at(c, layer, h, final), split_at(q, layer, h, final), layer)
                    if layer == 2 and g and g % (SECTION // GT) == 0:
                        release(c, g - 1, final)
                dve.wait_ge(stack_low, c * 2 + layer)
                nc.vector.tensor_tensor(stack_raw[:, :], bc[:, T1 - 1, :], x[:, :], ALU.mult).then_inc(stack_ready, 1)
                for h in pending:
                    low_part(split_at(c, layer, h, final), split_at(q, layer, h, final), layer)
                if layer == 2:
                    dve.wait_ge(stack_ready, c * 2 + 4)
                    dve.sem_inc(bc_free, 1)

            def release(c, g, final):
                for h in (g - 1, g):
                    if h < g and is_split(2, h) == is_split(2, g):
                        continue
                    if is_split(2, h):
                        dve.wait_ge(raw_ready, split_at(c, 2, h, final) + 1)
                    else:
                        dve.wait_ge(whole_ready, whole_at(c, 2, h, final) + 1)
                dve.sem_inc(bc_free, 1)

            def body(i, last):
                for q in range(BODY):
                    c = i * BODY + q
                    final = last and q == BODY - 1
                    field_products(i, q, 1, final, lambda: None)

                    def rotations_read():
                        dve.wait_ge(whole_ready, whole_at(c, 0, G0 - 1) + 1)
                        if S0:
                            dve.wait_ge(raw_ready, split_before(c) + S0)
                        dve.sem_inc(rot_free, 1)

                    if not final:
                        layer0_products(whole_at(c, 0, FIRST_WHOLE), whole_at(q, 0, FIRST_WHOLE),
                                        split_before(c), split_before(q), c + 2)
                    field_products(i, q, 2, final, (lambda: None) if final else rotations_read)

            layer0_products(0, 0, 0, 0, 1)
            dve.wait_ge(whole_ready, G0 - S0)
            dve.sem_inc(rot_free, 1)
            with dve.Fori(0, LOOPS - 1) as i:
                body(i, False)
            body(LOOPS - 1, True)

        @block.tensor
        def _(pe):
            def transposes(c, first=False):
                pe.wait_ge(gathered, (c + 1) * (16 * GATHERS))
                if not first:
                    pe.wait_ge(xt_ready, c * 2)
                nc.tensor.transpose(tp[:, 0:PART], emb[:, 0:PART], ident[:, :])
                rest = GATHERS * DIM - PART
                nc.tensor.transpose(tp[0:rest, PART:2 * PART], emb[:, PART:PART + rest], ident[:, :]).then_inc(transposed, 1)

            def split_group(count, k, layer, g):
                pe.wait_ge(low_ready, count + (1 + RAW_SLOTS))
                m, k = ROWS[layer], k % PART_SLOTS
                for u in range(GT):
                    n, out_z = PARTS_AT[layer, g] + u, z[layer][:, :]
                    nc.tensor.matmul(out_z, w_high[0:m, n, :], high[0:m, k, u], start=(g == 0 and u == 0), stop=False)
                    nc.tensor.matmul(out_z, w_low[0:m, n, :], high[0:m, k, u], start=False, stop=False)
                    ins = nc.tensor.matmul(out_z, w_high[0:m, n, :], low[0:m, k, u], start=False, stop=False)
                ins.then_inc(parts_free, 1)

            def layer0(whole_count, whole_k, split_count, split_k, c):
                pe.wait_ge(z_read[0], c + 1)
                w = n = 0
                for g in range(G0):
                    if is_split(0, g):
                        split_group(split_count + n, split_k + n, 0, g)
                        n += 1
                        continue
                    slot = (whole_k + w) % WHOLE_SLOTS
                    pe.wait_ge(whole_ready, whole_count + (w + 1))
                    w += 1
                    for t in range(GT * g, min(T0, GT * g + GT)):
                        k = ROWS0 if t < T0 - 1 else LAST0
                        ins = nc.tensor.matmul(z[0][:, :], w0[0:k, t, :], whole[0:k, slot, t - GT * g], start=(t == 0), stop=(t == T0 - 1))
                    ins.then_inc(whole_free, 1)

            def fields_layer(i, q, layer, w, final, gathers=False):
                c = i * BODY + q
                out_z = z[layer][:, :]
                pe.wait_ge(z_read[layer], c + 1)
                for g in range(G1):
                    if gathers and g == AHEAD:
                        transposes(c + 2)
                    if is_split(layer, g):
                        split_group(split_at(c, layer, g, final), split_at(q, layer, g, final), layer, g)
                    else:
                        pe.wait_ge(whole_ready, whole_at(c, layer, g, final) + 1)
                        slot = whole_at(q, layer, g, final) % WHOLE_SLOTS
                        for t in range(GT * g, min(T1 - 1, GT * g + GT)):
                            ins = nc.tensor.matmul(out_z, w[:, t, :], whole[:, slot, t - GT * g], start=(t == 0), stop=False)
                        ins.then_inc(whole_free, 1)
                n = GT * SPLIT_CHUNK + layer - 1
                pe.wait_ge(stack_low, c * 2 + (layer + 1))
                nc.tensor.matmul(out_z, w_high[:, n, :], stack[:, :], start=False, stop=False)
                nc.tensor.matmul(out_z, w_low[:, n, :], stack[:, :], start=False, stop=True).then_inc(stack_free, 1)

            def body(i, last):
                for q in range(BODY):
                    c = i * BODY + q
                    final = last and q == BODY - 1
                    fields_layer(i, q, 1, w1, final)
                    if not final:
                        layer0(whole_at(c, 0, FIRST_WHOLE), whole_at(q, 0, FIRST_WHOLE), split_before(c), split_before(q), c + 1)
                    fields_layer(i, q, 2, w2, final, not (last and q >= BODY - 2))

            for layer in range(3):
                pe.sem_inc(z_read[layer], 1)
            pe.wait_ge(ident_ready, 1)
            pe.wait_ge(small_in, 64)
            for j in range(BATCH // PART):
                ins = nc.tensor.transpose(top[0][0:DENSE, j * PART:(j + 1) * PART], dense[:, j, :], ident[:, :])
            ins.then_inc(dense_t, 1)
            transposes(0, first=True)
            pe.wait_ge(w0_ready, 2)
            pe.wait_ge(w12_in, 96)
            pe.wait_ge(w_split, 2 * len(split_weights))
            layer0(0, 0, 0, 0, 0)
            transposes(1)
            with pe.Fori(0, LOOPS - 1) as i:
                body(i, False)
            body(LOOPS - 1, True)

            pe.wait_ge(top_in, 16 * 6)
            pe.wait_ge(dense_ready, 1)
            pe.wait_ge(xt_ready, 2 * CHUNKS)
            pe.wait_ge(z_read[0], CHUNKS + 1)
            for m in range(H1 // PART):
                nc.tensor.matmul(h1_banks[m][:, :], wt1_dense[:, m * PART:(m + 1) * PART], denseT[:, :], start=True, stop=False)
            for at, width, chunks in ((0, BATCH - SUB, CHUNKS - 1), (BATCH - SUB, SUB, CHUNKS)):
                pe.wait_ge(summed, chunks * 4 + 1)
                for m in range(H1 // PART):
                    for t in range(2):
                        ins = nc.tensor.matmul(h1_banks[m][:, at:at + width], wt1[:, t, m * PART:(m + 1) * PART], logits[:, t, at:at + width],
                                               start=False, stop=(chunks == CHUNKS and t == 1))
                    if chunks == CHUNKS:
                        ins.then_inc(h1_done, 1)
            for layer in (1, 2):
                pe.wait_ge(z_read[layer], CHUNKS + 1)
            for t in range(H1 // PART):
                pe.wait_ge(h1_ready, t + 1)
                for m in range(H2 // PART):
                    ins = nc.tensor.matmul(z[1 + m][:, :], wt2[:, t, m * PART:(m + 1) * PART], h1[:, t, :], start=(t == 0), stop=(t == H1 // PART - 1))
                    if t == H1 // PART - 1:
                        ins.then_inc(h2_done, 1)
            pe.wait_ge(stack_ready, CHUNKS * 2 + 2)
            for t in range(H2 // PART):
                pe.wait_ge(h2_ready, t + 1)
                ins = nc.tensor.matmul(xk[0][0:1, :], wt3[:, t:t + 1], h2[:, t, :], start=(t == 0), stop=(t == H2 // PART - 1))
            ins.then_inc(y_done, 1)


def kernel(**inputs):
    import numpy as _np
    import concourse.bacc as _bacc
    from concourse import mybir as _mybir
    from concourse.bass_utils import run_bass_kernel_spmd as _run

    nc = _bacc.Bacc("TRN2", target_bir_lowering=False, num_devices=1)
    given = {k: _np.ascontiguousarray(v) for k, v in inputs.items() if k not in ("L0_rec_w0", "ids") and not k.startswith("tbl_")}
    tables = [_np.asarray(inputs[f"tbl_{f}"]) for f in range(FIELDS)]
    given["tables"] = _np.concatenate(tables, axis=0)
    starts = [0]
    for t in tables:
        starts.append(starts[-1] + t.shape[0])
    ids = _np.zeros((BY * GATHERS, BATCH), _np.int32)
    ids[0:FIELDS] = _np.asarray(inputs["ids"]).T
    given["ids"] = _np.ascontiguousarray(ids.reshape(BY, GATHERS, CHUNKS, SUB).transpose(0, 3, 2, 1).reshape(PART, CHUNKS, GATHERS))
    base = _np.zeros(BY * GATHERS, _np.int32)
    base[0:FIELDS] = starts[0:FIELDS]
    given["base"] = _np.repeat(base.reshape(BY, GATHERS), SUB, axis=0)
    w0 = _np.asarray(inputs["L0_rec_w0"])
    r, i = _np.arange(ROT)[:, None], _np.arange(FIELDS)[None, :]
    j = (i + r) % FIELDS
    given["w0_fwd"] = _np.ascontiguousarray(w0[i + 0 * r, j].reshape(ROT * FIELDS, OUT))
    rev = w0[j, i + 0 * r].reshape(ROT * FIELDS, OUT).copy()
    rev[0:FIELDS] = 0
    given["w0_rev"] = rev
    arrays, aps = {}, {}
    for name, a in given.items():
        arrays["in_" + name] = a
        aps[name] = nc.dram_tensor("in_" + name, a.shape, _mybir.dt.from_np(a.dtype), kind="ExternalInput").ap()
    fields = nc.dram_tensor("fields", (CHUNKS * (FIELDS + WRAP) * N,), _mybir.dt.float32).ap()
    out = nc.dram_tensor("out_y", (BATCH, 1), _mybir.dt.float32, kind="ExternalOutput").ap()
    tower(nc, aps, fields, out)
    result = _run(nc, [arrays], core_ids=[0])
    return result.results[0]["out_y"]
```
